# Optimizing a Trainium2 kernel written in Bass

```python
import numpy as np
import jax
import jax.numpy as jnp

def _softmax(x, axis=-1):
    return jax.nn.softmax(x, axis=axis)

def _gelu(x):
    return jax.nn.gelu(x, approximate=True)

def _silu(x):
    return jax.nn.silu(x)

def _sigmoid(x):
    return jax.nn.sigmoid(x)

def _layernorm(x, axis=-1, eps=1e-05):
    m = jnp.mean(x, axis=axis, keepdims=True)
    v = jnp.var(x, axis=axis, keepdims=True)
    return (x - m) / jnp.sqrt(v + eps)

def _scatter_add(tgt, idx, src, axis=0):
    return tgt.at[idx].add(src)

def _segment_sum(src, seg, n):
    return jax.ops.segment_sum(src, seg, n)
kernel_name = 'mk_audio_tower_d1_tok_audfeat512_r4_936d05'

def setup_inputs(seed: int=0):
    np.random.seed(seed)
    _w = jnp.asarray

    def _rec_inputs():
        import jax
        import jax.numpy as jnp
        _rk = jax.random.key(seed)
        x = -0.000520686 + 1.00062 * jax.random.normal(jax.random.fold_in(_rk, 1), (64, 32, 250), jnp.float32)
        return x
    x = _rec_inputs()

    def _L0_tok_setup():
        import jax, jax.numpy as jnp
        import numpy as np
        ALPHA = 0.1

        def ewma(y, alpha=ALPHA):
            y_t = jnp.swapaxes(y, 0, 1)

            def step(carry, xt):
                c = alpha * xt + (1.0 - alpha) * carry
                return (c, c)
            _, out = jax.lax.scan(step, y_t[0], y_t[1:])
            out = jnp.concatenate([y_t[:1], out], axis=0)
            return jnp.swapaxes(out, 0, 1)
        key = jax.random.key(seed)
        k1, k2, k3, k4, k5 = jax.random.split(key, 5)
        B, C, T, D = (32, 32, 512, 128)
        x = jax.random.normal(k1, (B, C, T), dtype=jnp.float32)
        W_ve = jax.random.normal(k2, (D, C), dtype=jnp.float32) * (1.0 / np.sqrt(C))
        b_ve = jax.random.normal(k3, (D,), dtype=jnp.float32) * 0.01
        W_lin = jax.random.normal(k4, (D, D), dtype=jnp.float32) * (1.0 / np.sqrt(D))
        b_lin = jax.random.normal(k5, (D,), dtype=jnp.float32) * 0.01
        return {'x': x, 'W_ve': W_ve, 'b_ve': b_ve, 'W_lin': W_lin, 'b_lin': b_lin}
    _L0_tok_all = _L0_tok_setup()
    _L0_tok_in = {k: v for k, v in _L0_tok_all.items() if k in ('W_ve', 'b_ve', 'W_lin', 'b_lin')}
    del _L0_tok_all

    def _L0_attn_setup():
        import jax, jax.numpy as jnp
        import numpy as np
        import math
        B, S, H = (2, 1024, 128)
        NUM_HEADS = 8
        HEAD_DIM = H // NUM_HEADS
        RECENCY_DECAY = 0.9
        key = jax.random.key(seed)
        k1, k2, k3 = jax.random.split(key, 3)
        scale = 1.0 / math.sqrt(H)
        x = jax.random.normal(k1, (B, S, H), dtype=jnp.float32)
        w_qkv = jax.random.normal(k2, (3 * H, H), dtype=jnp.float32) * scale
        w_out = jax.random.normal(k3, (H, H), dtype=jnp.float32) * scale
        b_out = jnp.zeros((H,), dtype=jnp.float32)
        return {'x': x, 'w_qkv': w_qkv, 'w_out': w_out, 'b_out': b_out}
    _L0_attn_all = _L0_attn_setup()
    _L0_attn_in = {k: v for k, v in _L0_attn_all.items() if k in ('w_qkv', 'w_out', 'b_out')}
    del _L0_attn_all

    def _L0_ffn_setup():
        import jax, jax.numpy as jnp
        import numpy as np
        B, S, D = (32, 128, 128)
        E, H, O, K = (8, 512, 128, 2)
        key = jax.random.key(seed)
        ks = jax.random.split(key, 5)
        sc = lambda k, shape, scale: jax.random.normal(k, shape, jnp.float32) * scale
        return {'x': sc(ks[0], (B, S, D), 1.0), 'attn_w': sc(ks[1], (D, 1), 0.05), 'attn_b': jnp.zeros((1,), jnp.float32), 'gate_w': sc(ks[2], (D, E), 0.05), 'gate_b': jnp.zeros((E,), jnp.float32), 'w1': sc(ks[3], (E, D, H), 0.02), 'b1': jnp.zeros((E, H), jnp.float32), 'w2': sc(ks[4], (E, H, O), 0.02), 'b2': jnp.zeros((E, O), jnp.float32)}
    _L0_ffn_all = _L0_ffn_setup()
    _L0_ffn_in = {k: v for k, v in _L0_ffn_all.items() if k in ('attn_w', 'attn_b', 'gate_w', 'gate_b', 'w1', 'b1', 'w2', 'b2')}
    del _L0_ffn_all
    return {'x': x, 'L0_tok_W_ve': _L0_tok_in['W_ve'], 'L0_tok_b_ve': _L0_tok_in['b_ve'], 'L0_tok_W_lin': _L0_tok_in['W_lin'], 'L0_tok_b_lin': _L0_tok_in['b_lin'], 'L0_attn_w_qkv': _L0_attn_in['w_qkv'], 'L0_attn_w_out': _L0_attn_in['w_out'], 'L0_attn_b_out': _L0_attn_in['b_out'], 'L0_ffn_attn_w': _L0_ffn_in['attn_w'], 'L0_ffn_attn_b': _L0_ffn_in['attn_b'], 'L0_ffn_gate_w': _L0_ffn_in['gate_w'], 'L0_ffn_gate_b': _L0_ffn_in['gate_b'], 'L0_ffn_w1': _L0_ffn_in['w1'], 'L0_ffn_b1': _L0_ffn_in['b1'], 'L0_ffn_w2': _L0_ffn_in['w2'], 'L0_ffn_b2': _L0_ffn_in['b2']}

def reference(x, L0_tok_W_ve, L0_tok_b_ve, L0_tok_W_lin, L0_tok_b_lin, L0_attn_w_qkv, L0_attn_w_out, L0_attn_b_out, L0_ffn_attn_w, L0_ffn_attn_b, L0_ffn_gate_w, L0_ffn_gate_b, L0_ffn_w1, L0_ffn_b1, L0_ffn_w2, L0_ffn_b2):
    import jax
    import jax.numpy as jnp

    def _L0_tok_ref(x, W_ve, b_ve, W_lin, b_lin):
        import jax, jax.numpy as jnp
        import numpy as np
        ALPHA = 0.1

        def ewma(y, alpha=ALPHA):
            y_t = jnp.swapaxes(y, 0, 1)

            def step(carry, xt):
                c = alpha * xt + (1.0 - alpha) * carry
                return (c, c)
            _, out = jax.lax.scan(step, y_t[0], y_t[1:])
            out = jnp.concatenate([y_t[:1], out], axis=0)
            return jnp.swapaxes(out, 0, 1)
        xt = jnp.transpose(x, (0, 2, 1))
        B, T, C = xt.shape
        x_diff = jnp.concatenate([jnp.zeros((B, 1, C), dtype=xt.dtype), xt[:, 1:, :] - xt[:, :-1, :]], axis=1)
        x_emb = jnp.einsum('btc,dc->btd', x_diff, W_ve) + b_ve
        x_lr = ewma(x_emb)
        x_rl = jnp.flip(ewma(jnp.flip(x_emb, axis=1)), axis=1)
        x_smooth = (x_lr + x_rl) * 0.5
        return jnp.einsum('btd,ed->bte', x_smooth, W_lin) + b_lin

    def _L0_attn_ref(x, w_qkv, w_out, b_out):
        import jax, jax.numpy as jnp
        import numpy as np
        import math
        B, S, H = (2, 1024, 128)
        NUM_HEADS = 8
        HEAD_DIM = H // NUM_HEADS
        RECENCY_DECAY = 0.9
        batch, seq_len, hidden = x.shape
        nh, hd = (NUM_HEADS, HEAD_DIM)
        qkv = jnp.einsum('bsh,oh->bso', x, w_qkv)
        qkv = qkv.reshape(batch, seq_len, 3, nh, hd)
        q, k, v = jnp.transpose(qkv, (2, 0, 3, 1, 4))
        attn = jnp.einsum('bhqd,bhkd->bhqk', q, k) / math.sqrt(hd)
        pos = jnp.arange(seq_len)[None, :] - jnp.arange(seq_len)[:, None]
        bias = jnp.where(pos <= 0, pos.astype(jnp.float32) * math.log(RECENCY_DECAY), jnp.zeros((), dtype=jnp.float32))
        attn = jax.nn.softmax(attn + bias[None, None, :, :], axis=-1)
        out = jnp.einsum('bhqk,bhkd->bqhd', attn, v).reshape(batch, seq_len, hidden)
        return jnp.einsum('bsh,oh->bso', out, w_out) + b_out

    def _L0_ffn_ref(x, attn_w, attn_b, gate_w, gate_b, w1, b1, w2, b2):
        import jax, jax.numpy as jnp
        import numpy as np
        B, S, D = (32, 128, 128)
        E, H, O, K = (8, 512, 128, 2)
        scores = x @ attn_w + attn_b
        aw = jax.nn.softmax(scores, axis=1)
        pooled = jnp.sum(x * aw, axis=1)
        gates = jax.nn.softmax(pooled @ gate_w + gate_b, axis=-1)
        _, idx = jax.lax.top_k(gates, K)
        mask = jnp.sum(jax.nn.one_hot(idx, E, dtype=gates.dtype), axis=-2)
        g = gates * mask
        g = g / (jnp.sum(g, axis=-1, keepdims=True) + 1e-09)
        h = jax.nn.gelu(jnp.einsum('bsd,edh->ebsh', x, w1) + b1[:, None, None, :], approximate=False)
        eo = jax.nn.gelu(jnp.einsum('ebsh,eho->ebso', h, w2) + b2[:, None, None, :], approximate=False)
        return jnp.einsum('ebso,be->bso', eo, g)
    h = _L0_tok_ref(x, L0_tok_W_ve, L0_tok_b_ve, L0_tok_W_lin, L0_tok_b_lin)
    h = h + _L0_attn_ref(_layernorm(h, axis=-1), L0_attn_w_qkv, L0_attn_w_out, L0_attn_b_out)
    h = h + _L0_ffn_ref(_layernorm(h, axis=-1), L0_ffn_attn_w, L0_ffn_attn_b, L0_ffn_gate_w, L0_ffn_gate_b, L0_ffn_w1, L0_ffn_b1, L0_ffn_w2, L0_ffn_b2)
    return h

_drawn_inputs = setup_inputs


def setup_inputs(seed=0):
    import zlib

    import numpy as np

    out = dict(_drawn_inputs(seed))
    spreads = {'L0_attn_b_out': (0.0, 0.1),
     'L0_ffn_gate_b': (0.0, 0.1),
     'L0_ffn_b1': (0.0, 0.42),
     'L0_ffn_b2': (0.0, 0.1)}
    factors = {'L0_ffn_attn_w': 4.488}
    for name, (base, spread) in spreads.items():
        noise = np.random.default_rng([zlib.crc32(name.encode()), seed]).standard_normal(out[name].shape)
        drawn = base * np.exp(spread * noise) if base else spread * noise
        out[name] = jnp.asarray(drawn.astype(out[name].dtype))
    for name, factor in factors.items():
        out[name] = (out[name] * factor).astype(out[name].dtype)
    return out
```

```python
import math
from contextlib import ExitStack

import numpy as np

import concourse.bass as bass
from concourse import mybir

F32 = mybir.dt.float32
BF16 = mybir.dt.bfloat16
U32 = mybir.dt.uint32
ALU = mybir.AluOpType
ACT = mybir.ActivationFunctionType
AX_X = mybir.AxisListType.X

B, C, T = 64, 32, 250
D = 128
NH, HD = 8, 16
E, HID, TOPK = 8, 512, 2
P = 125
NT = T // P
U = 4
G = B // U
HC = HID // D
VW = HD + 1
RING = 4

ALPHA = 0.1
LAMBDA = -math.log(0.9)
Q_SCALE = 1.0 / (math.sqrt(HD) * LAMBDA)
EPS = 1e-5

ROW_K, ROW_1, ROW_M = 3 * HD, 3 * HD + 1, 3 * HD + 2
STACK_DMAS = 4
ROWS_DOT, ROWS_ALL, HALF = 3 * HD, 3 * HD + 4, 64


def constants():
    k = np.arange(P)[:, None]
    q = np.arange(P)[None, :]
    ident = np.eye(D, dtype=np.float32)
    diag = np.zeros((D, NT, P), np.float32)
    diag[:P, 0] = np.maximum(k - q, 0)
    diag[:P, 1] = np.maximum(q - k, 0)
    qrows = np.zeros((D, T), np.float32)
    krows = np.zeros((D, T), np.float32)
    for half in range(2):
        r = HALF * half
        krows[r + ROW_K, :P] = -np.arange(P)
        qrows[r + ROW_K] = 1
        krows[r + ROW_1, :P] = 1
        qrows[r + ROW_1] = np.arange(T)
        krows[r + ROW_M:r + ROW_M + 2] = -1
    return np.ascontiguousarray(np.concatenate([ident, diag.reshape(D, -1), qrows, krows], axis=1))


class Row:

    def __init__(self, first, u):
        self.first, self.u = first, u

    def plus(self, k):
        carry, u = divmod(self.u + k, U)
        return Row(self.first + U * carry if carry else self.first, u)

    @property
    def static(self):
        return isinstance(self.first, int)

    def count(self, each=1, upto=None):
        upto = each if upto is None else upto
        return self.first * each + (self.u * each + upto)

    @property
    def index(self):
        return self.first + self.u if self.u or self.static else self.first

    @property
    def exists(self):
        return not self.static or 0 <= self.first + self.u < B

    def after(self, k):
        return not self.static or self.first + self.u - k >= 0


def run_pipeline(eng, iteration):
    for i in range(-2, U):
        iteration(Row(0, 0).plus(i))
    with eng.Fori(U, B - U, U) as first:
        for u in range(U):
            iteration(Row(first, u))
    for i in range(B - U, B + 1):
        iteration(Row(0, 0).plus(i))


def attention_phase(nc, h_all, xt_all, sg_all, consts, x, W_ve, W_lin_T, b_ve, b_lin, w_qkv_T,
                    w_out_T, b_out, attn_w, gate_w):
    with ExitStack() as ctx:
        def sb(name, shape, dt=F32):
            return ctx.enter_context(nc.sbuf_tensor(name, shape, dt))

        def sem(name):
            return ctx.enter_context(nc.semaphore(name))

        def bank(name):
            return ctx.enter_context(nc.psum_tensor(name, [D, 512], F32))

        ps_s = [bank(f"ps_s{i}") for i in range(2)]
        ps_st = [bank(f"ps_st{i}") for i in range(2)]
        ps_in = bank("ps_in")
        ps_qk = bank("ps_qk")
        ps_o = bank("ps_o")
        ps_tail = bank("ps_tail")

        const = sb("const", [D, D + NT * P + 2 * T])
        identf = const[:, 0:D]
        identb = sb("identb", [D, D], BF16)
        diag = sb("diag", [D, NT, P], BF16)
        stacks = sb("stacks", [D, RING, 2, NH // 2, T], BF16)
        x_raw = sb("x_raw", [D, T])
        x_diff = sb("x_diff", [D, T])
        x_step = sb("x_step", [D, T])
        x_left = sb("x_left", [D, T])
        x_right = sb("x_right", [D, T])
        x_smooth = sb("x_smooth", [D, T])
        keep = sb("keep", [D, T])
        w_emb = sb("w_emb", [D, D])
        w_ve4 = sb("w_ve4", [D, U * C])
        w_linT = sb("w_linT", [D, D])
        b_ve_col = sb("b_ve_col", [D, 1])
        b_ve_wide = sb("b_ve_wide", [D, D])
        bias_in = sb("bias_in", [D, D])
        b_lin_row = sb("b_lin_row", [D, D])
        b_out_row = sb("b_out_row", [D, D])
        wf = sb("wf", [D, 4 * D])
        wq = sb("wq", [D, D])
        wh = sb("wh", [D, 4, D], BF16)
        wl = sb("wl", [D, 4, D], BF16)
        wrf = sb("wrf", [D, 1 + E])
        wrh = sb("wrh", [D, 1 + E], BF16)
        wrl = sb("wrl", [D, 1 + E], BF16)
        power = sb("power", [D, NT])
        h_raw = sb("h_raw", [D, NT * D])
        h_in = sb("h_in", [D, NT * D])
        h_res = sb("h_res", [D, RING, NT * D])
        st1 = sb("st1", [D, NT, 6])
        mv1 = sb("mv1", [D, NT, 2])
        ve1 = sb("ve1", [D, NT])
        rs1 = sb("rs1", [D, NT])
        xn1 = sb("xn1", [D, NT, D])
        x1h = sb("x1h", [D, T], BF16)
        x1l = sb("x1l", [D, T], BF16)
        parts = sb("parts", [D, 2, 4, T], BF16)
        v_sb = sb("v_sb", [D, RING, NT, NH, VW])
        mx = sb("mx", [D, NH * NT])
        mxp = sb("mxp", [D, 2, 2, NH], BF16)
        mxt = sb("mxt", [4 * NH, P], BF16)
        pt = sb("pt", [D, RING, NT, T])
        o_rec = sb("o_rec", [D, NT, NH])
        o_n = sb("o_n", [D, NT, NH, HD])
        oth = sb("oth", [D, T], BF16)
        otl = sb("otl", [D, T], BF16)
        h2 = sb("h2", [D, NT * D])
        st2 = sb("st2", [D, NT, 6])
        mv2 = sb("mv2", [D, NT, 2])
        ve2 = sb("ve2", [D, NT])
        rs2 = sb("rs2", [D, NT])
        xn2 = sb("xn2", [D, NT, D])
        x2h = sb("x2h", [D, T], BF16)
        x2l = sb("x2l", [D, T], BF16)

        scratch = [nc.dram_tensor(f"scratch{i}", (6, D, T), BF16, kind="Internal").ap() for i in range(2)]

        s_parts = [sem(f"parts_in_dram{i}") for i in range(RING)]
        s_const, s_w, s_x = sem("consts_loaded"), sem("weights_loaded"), sem("x_loaded")
        s_stack = [sem(f"stack_in_place{i}") for i in range(RING)]
        s_mrow = [sem(f"max_rows_in_place{i}") for i in range(RING)]
        s_prep, s_pv, s_pw = sem("prepared_vector"), sem("prepared_pool"), sem("embedding_product")
        s_keep, s_wv = sem("vector_constants"), sem("weights_split")
        s_diff, s_scan, s_smooth = sem("x_diff_made"), sem("x_scans"), sem("x_smoothed")
        s_half = sem("x_sums")
        (s_emb, s_hraw, s_hin, s_hres, s_st1, s_ag1, s_ve1, s_rs1, s_xn1, s_x1t, s_x1h, s_x1l, s_qk,
         s_qkh, s_qkl, s_v, s_vsb) = (sem(n) for n in (
            "embedded", "embedding_out", "bias_added", "residual_kept", "stats1", "aggr1", "var1",
            "rstd1", "norm1", "norm1_turned", "norm1_hi", "norm1_lo", "qk_product", "qk_hi", "qk_lo",
            "v_product", "v_out"))
        (s_s, s_max, s_mt, s_mh, s_ml, s_st, s_exp, s_pvp) = (sem(n) for n in (
            "scores", "score_max", "max_turned", "max_hi", "max_lo", "scores_t", "exp_done",
            "pv_product"))
        s_mrow_made = sem("max_rows_made")
        (s_rec, s_on, s_ot, s_oth, s_otl, s_prj, s_h2, s_st2, s_ag2, s_ve2, s_rs2, s_xn2, s_x2t,
         s_x2h, s_x2l, s_sg, s_sgo, s_hst, s_xst) = (sem(n) for n in (
            "recip", "o_normed", "o_turned", "o_hi", "o_lo", "o_projected", "h2_made", "stats2",
            "aggr2", "var2", "rstd2", "norm2", "norm2_turned", "norm2_hi", "norm2_lo",
            "router_product", "router_out", "h2_stored", "norm2_stored"))

        def head(which, row, h, rows, lo, n):
            r = HALF * (h % 2)
            return stacks[r:r + rows, row.u, which, h // 2, lo:lo + n]

        def dma_count(row, each):
            return 16 * each * (row.first // U + 1) if row.static else row.first * (16 * each // U) + 16 * each

        def x_group(first):
            return x.rearrange("(g q) c t -> g (q c) t", q=U)[first]

        ps_max = ps_tail[:, 0:P].bitcast(BF16)[:, 0:P]

        block = ctx.enter_context(nc.Block())

        @block.sync
        def _(sp):
            sp.dma_start(const[:], consts).then_inc(s_const, 16)
            sp.dma_start(x_raw[:], x_group(0)).then_inc(s_x, 16)
            sp.dma_start(w_ve4[:].rearrange("p (q c) -> p q c", q=U),
                         W_ve.rearrange("d (o c) -> d o c", o=1).broadcast_to([D, U, C])).then_inc(s_w, 16)
            sp.dma_start(w_linT[:], W_lin_T).then_inc(s_w, 16)
            sp.dma_start(b_ve_col[:], b_ve.rearrange("(d o) -> d o", o=1)).then_inc(s_w, 16)
            sp.dma_start(b_lin_row[:], b_lin.partition_broadcast(D)).then_inc(s_w, 16)
            sp.dma_start(b_out_row[:], b_out.partition_broadcast(D)).then_inc(s_w, 16)
            sp.dma_start(wf[:, 0:3 * D], w_qkv_T).then_inc(s_w, 16)
            sp.dma_start(wf[:, 3 * D:4 * D], w_out_T).then_inc(s_w, 16)
            sp.dma_start(wrf[:, 0:1], attn_w).then_inc(s_w, 16)
            sp.dma_start(wrf[:, 1:1 + E], gate_w).then_inc(s_w, 16)
            sp.wait_ge(s_keep, 2 + 2 * RING)

            def max_rows(row):
                sp.wait_ge(s_mrow_made, row.count())
                for half in range(2):
                    r = HALF * half + ROW_M
                    sp.dma_start(stacks[r:r + 2, row.u, 0, :, :].rearrange("r h (t p) -> r (h t) p", t=NT),
                                 mxt[2 * NH * half:2 * NH * (half + 1), :]).then_inc(s_mrow[row.u], 16)

            def stack(row):
                sp.wait_ge(s_qkh, row.count())
                sp.wait_ge(s_qkl, row.count())
                place = scratch[row.u % 2]
                for first in range(3):
                    sp.dma_start(place[2 * first:2 * first + 2].rearrange("g p t -> p g t"),
                                 parts[:, row.u % 2, first:first + 2, :]).then_inc(s_parts[row.u], 16)
                sp.wait_ge(s_parts[row.u], dma_count(row, 3))
                for which in range(2):
                    for half in range(2):
                        src = place[3 * which:3 * which + 3, D // 2 * half:D // 2 * (half + 1), :]
                        sp.dma_start(stacks[HALF * half:HALF * half + ROWS_DOT, row.u, which, :, :],
                                     src.rearrange("g (d h) t -> g d (h t)", d=HD)).then_inc(s_stack[row.u], 16)

            def iteration(i):
                new, mid = i.plus(2), i.plus(1)
                if new.exists:
                    stack(new)
                if mid.exists:
                    max_rows(mid)
                if new.exists and new.u == U - 1 and (not new.static or new.first + U < B):
                    group = new.first // U if new.static else None
                    if new.static:
                        sp.wait_ge(s_diff, 2 * (group + 1))
                        sp.dma_start(x_raw[:], x_group(group + 1)).then_inc(s_x, 16)
                    else:
                        sp.wait_ge(s_diff, new.first // 2 + 2)
                        nxt = new.first // U + 1
                        sp.dma_start(x_raw[:], x_group(nxt)).then_inc(s_x, 16)

            run_pipeline(sp, iteration)

        @block.gpsimd
        def _(pool):
            pool.memset(power[:], -0.5).then_inc(s_pv, 1)
            pool.memset(v_sb[:], 1.0).then_inc(s_pv, 1)
            pool.wait_ge(s_pv, 2)
            pool.wait_ge(s_pw, 3)

            def embed_out(row):
                pool.wait_ge(s_hraw, row.count())
                if row.after(1):
                    pool.wait_ge(s_xn1, row.plus(-1).count(NT))
                for t in range(NT):
                    last = pool.tensor_tensor(h_in[0:P, t * D:(t + 1) * D], h_raw[0:P, t * D:(t + 1) * D],
                                              bias_in[0:P, :], ALU.add)
                last.then_inc(s_hin, 1)
                pool.wait_ge(s_hin, row.count())
                for t in range(NT):
                    last = pool.tensor_tensor(h_res[0:P, row.u, t * D:(t + 1) * D],
                                              h_in[0:P, t * D:(t + 1) * D], b_out_row[0:P, :], ALU.add)
                last.then_inc(s_hres, 1)

            def rstd(row, var, rs, s_in, s_outp, s_read):
                pool.wait_ge(s_in, row.count())
                pool.tensor_tensor(rs[0:P, :], var[0:P, :], power[0:P, :], ALU.pow).then_inc(s_outp, 1)

            def store(row):
                pool.wait_ge(s_h2, row.count())
                pool.tensor_copy(h_all[0:P, row.index, :], h2[0:P, :]).then_inc(s_hst, 1)

            def store_turned(row):
                pool.wait_ge(s_x2h, row.count())
                pool.tensor_copy(xt_all[:, row.index, 0, :], x2h[:])
                pool.wait_ge(s_x2l, row.count())
                pool.tensor_copy(xt_all[:, row.index, 1, :], x2l[:]).then_inc(s_xst, 1)

            def iteration(i):
                new, old = i.plus(2), i.plus(-1)
                if new.exists:
                    embed_out(new)
                    rstd(new, ve1, rs1, s_ve1, s_rs1, s_xn1)
                if old.exists:
                    rstd(old, ve2, rs2, s_ve2, s_rs2, s_xn2)
                    store(old)
                    store_turned(old)

            run_pipeline(pool, iteration)

        @block.scalar
        def _(act):
            def embed_out(row):
                act.wait_ge(s_emb, row.count())
                if row.after(1):
                    act.wait_ge(s_hin, row.plus(-1).count())
                act.copy(h_raw[0:P, :], ps_in[0:P, 0:NT * D]).then_inc(s_hraw, 1)

            def norm1_hi(row):
                act.wait_ge(s_x1t, row.count())
                act.copy(x1h[:], ps_in[:, 0:T]).then_inc(s_x1h, 1)

            def qk_hi(row):
                act.wait_ge(s_qk, row.count())
                if row.after(2):
                    act.wait_ge(s_stack[(row.u + 2) % RING], dma_count(row.plus(-2), STACK_DMAS))
                act.copy(parts[:, row.u % 2, 1:3, :], ps_qk[:, 0:2 * T].rearrange("p (a t) -> p a t", a=2)).then_inc(s_qkh, 1)

            def v_out(row):
                act.wait_ge(s_v, row.count())
                act.copy(v_sb[0:P, row.u, :, :, 0:HD],
                         ps_in[0:P, 0:NT * D].rearrange("p (t h d) -> p t h d", t=NT, h=NH)).then_inc(s_vsb, 1)

            def exps(row, h):
                act.wait_ge(s_st, row.count(NH, h + 1))
                if h >= RING or row.after(1):
                    act.wait_ge(s_pvp, row.count(NH, h + 1 - RING))
                act.activation(pt[0:P, h % RING, :, :].rearrange("p a t -> p (a t)"),
                               ps_st[h % 2][0:P, 0:NT * T], ACT.Exp, scale=LAMBDA).then_inc(s_exp, 1)

            def max_out(row):
                act.wait_ge(s_mt, row.count())
                if row.after(1):
                    act.wait_ge(s_mrow[(row.u - 1) % RING], dma_count(row.plus(-1), 2))
                act.copy(mxt[:], ps_max[0:4 * NH, 0:P]).then_inc(s_mrow_made, 1)

            def o_hi(row):
                act.wait_ge(s_ot, row.count())
                act.copy(oth[:], ps_tail[:, 0:T]).then_inc(s_oth, 1)

            def norm2_hi(row):
                act.wait_ge(s_x2t, row.count())
                if row.after(1):
                    act.wait_ge(s_xst, row.plus(-1).count())
                act.copy(x2h[:], ps_tail[:, 0:T]).then_inc(s_x2h, 1)

            act.wait_ge(s_pv, 2)

            def iteration(i):
                new, mid, old = i.plus(2), i.plus(1), i.plus(-1)
                for h in range(NH):
                    if h == 0 and new.exists:
                        embed_out(new)
                    if i.exists:
                        exps(i, h)
                    if h == 2 and new.exists:
                        norm1_hi(new)
                    if h == 2 and old.exists:
                        o_hi(old)
                    if h == 3 and new.exists:
                        qk_hi(new)
                    if h == 5 and mid.exists:
                        max_out(mid)
                    if h == 5 and new.exists:
                        v_out(new)
                    if h == 6 and old.exists:
                        norm2_hi(old)

            run_pipeline(act, iteration)

        @block.vector
        def _(dve):
            dve.memset(keep[:], 1.0 - ALPHA).then_inc(s_prep, 1)
            dve.memset(x_diff[:, 0:1], 0.0).then_inc(s_prep, 1)
            dve.wait_ge(s_const, 16)
            dve.tensor_copy(identb[:], identf).then_inc(s_keep, 1)
            dve.tensor_copy(diag[:].rearrange("p a t -> p (a t)"), const[:, D:D + NT * P]).then_inc(s_keep, 1)
            for which in range(2):
                at = D + NT * P + which * T
                rows = const[:, at:at + T].rearrange("p (o t) -> p o t", o=1).broadcast_to([D, NH // 2, T])
                for r in range(RING):
                    dve.tensor_copy(stacks[:, r, which, :, :], rows).then_inc(s_keep, 1)
            dve.wait_ge(s_w, 16 * 9)
            dve.tensor_scalar(wq[:], wf[:, 0:D], Q_SCALE, None, ALU.mult).then_inc(s_wv, 1)
            dve.tensor_copy(wh[:, 1:4, :], wf[:, D:4 * D].rearrange("p (a d) -> p a d", a=3)).then_inc(s_wv, 1)
            dve.tensor_copy(wrh[:], wrf[:]).then_inc(s_wv, 1)
            dve.wait_ge(s_wv, 3)
            dve.tensor_copy(wh[:, 0, :], wq[:]).then_inc(s_wv, 1)
            dve.wait_ge(s_wv, 4)
            dve.tensor_tensor(wl[:, 0, :], wq[:], wh[:, 0, :], ALU.subtract).then_inc(s_wv, 1)
            dve.tensor_tensor(wl[:, 1:4, :], wf[:, D:4 * D].rearrange("p (a d) -> p a d", a=3),
                              wh[:, 1:4, :], ALU.subtract).then_inc(s_wv, 1)
            dve.tensor_tensor(wrl[:], wrf[:], wrh[:], ALU.subtract).then_inc(s_wv, 1)
            dve.tensor_scalar(b_ve_wide[:], identf, 0.0, b_ve_col[:, 0:1], ALU.mult, ALU.add).then_inc(s_wv, 1)
            dve.wait_ge(s_pw, 1)
            dve.tensor_copy(w_emb[:], ps_in[:, 0:D]).then_inc(s_pw, 1)
            dve.tensor_tensor(bias_in[:], ps_in[:, D:2 * D], b_lin_row[:], ALU.add).then_inc(s_pw, 1)

            def smooth(group, last_row):
                dve.wait_ge(s_x, group * 16 + 16)
                dve.wait_ge(s_scan, group * 2) if not isinstance(group, int) or group else None
                dve.tensor_tensor(x_diff[:, 1:T], x_raw[:, 1:T], x_raw[:, 0:T - 1], ALU.subtract).then_inc(s_diff, 1)
                dve.wait_ge(s_diff, group * 2 + 1)
                dve.tensor_scalar(x_step[:], x_diff[:], ALPHA, None, ALU.mult).then_inc(s_diff, 1)
                dve.wait_ge(s_diff, group * 2 + 2)
                dve.tensor_tensor_scan(x_left[:, 1:T], keep[:, 1:T], x_step[:, 1:T], x_diff[:, 0:1],
                                       ALU.mult, ALU.add).then_inc(s_scan, 1)
                dve.tensor_tensor_scan(x_right[:, T - 2::-1], keep[:, 1:T], x_step[:, T - 2::-1],
                                       x_diff[:, T - 1:T], ALU.mult, ALU.add).then_inc(s_scan, 1)
                dve.tensor_copy(x_left[:, 0:1], x_diff[:, 0:1])
                dve.tensor_copy(x_right[:, T - 1:T], x_diff[:, T - 1:T]).then_inc(s_half, 1)
                dve.wait_ge(s_scan, group * 2 + 2)
                dve.wait_ge(s_half, group * 2 + 1)
                dve.tensor_tensor(x_left[:], x_left[:], x_right[:], ALU.add).then_inc(s_half, 1)
                dve.wait_ge(s_half, group * 2 + 2)
                if last_row is not None:
                    dve.wait_ge(s_emb, last_row.count())
                dve.tensor_scalar(x_smooth[:], x_left[:], 0.5, None, ALU.mult).then_inc(s_smooth, 1)

            def score_max(row, h):
                dve.wait_ge(s_s, row.count(NH, h + 1))
                if h == 0 and row.after(1):
                    dve.wait_ge(s_ml, row.plus(-1).count())
                dve.tensor_reduce(mx[0:P, (h % 2 * (NH // 2) + h // 2) * NT:(h % 2 * (NH // 2) + h // 2 + 1) * NT],
                                  ps_s[h % 2][0:P, 0:NT * T].rearrange("p (a t) -> p a t", a=NT),
                                  AX_X, ALU.max).then_inc(s_max, 1)

            def stats(row, src, st, a):
                for t in range(NT):
                    dve.bn_stats(st[0:P, t, :], src[0:P, t * D:(t + 1) * D]).then_inc(a, 1)
                dve.wait_ge(a, row.count(NT))

            def aggregate(row, st, mv, ve, b, c):
                for t in range(NT):
                    dve.bn_aggr(mv[0:P, t, :], st[0:P, t, :]).then_inc(b, 1)
                dve.wait_ge(b, row.count(NT))
                dve.tensor_scalar(ve[0:P, :], mv[0:P, :, 1], EPS, None, ALU.add).then_inc(c, 1)

            def normed(row, src, mv, rs, xn, s_in, s_done):
                dve.wait_ge(s_in, row.count())
                for t in range(NT):
                    dve.tensor_scalar(xn[0:P, t, :], src[0:P, t * D:(t + 1) * D], mv[0:P, t, 0:1],
                                      rs[0:P, t:t + 1], ALU.subtract, ALU.mult).then_inc(s_done, 1)

            def low(row, dst, psum, hi, s_hi, s_lo):
                dve.wait_ge(s_hi, row.count())
                dve.tensor_tensor(dst, psum, hi, ALU.subtract).then_inc(s_lo, 1)

            def max_parts(row):
                dve.wait_ge(s_max, row.count(NH))
                if row.after(1):
                    dve.wait_ge(s_mt, row.plus(-1).count())
                m = mx[0:P, :].rearrange("p (a h) -> p a h", a=2)
                dve.tensor_copy(mxp[0:P, :, 0, :], m).then_inc(s_mh, 1)
                dve.wait_ge(s_mh, row.count())
                dve.tensor_tensor(mxp[0:P, :, 1, :], m, mxp[0:P, :, 0, :], ALU.subtract).then_inc(s_ml, 1)

            def o_normed(row):
                dve.wait_ge(s_pvp, row.count(NH))
                o = ps_o[0:P, 0:NT * NH * VW].rearrange("p (t h d) -> p t h d", t=NT, h=NH)
                dve.reciprocal(o_rec[0:P, :, :], o[:, :, :, HD]).then_inc(s_rec, 1)
                dve.wait_ge(s_rec, row.count())
                rec = o_rec[0:P, :, :].rearrange("p t (h o) -> p t h o", o=1).broadcast_to([P, NT, NH, HD])
                dve.tensor_tensor(o_n[0:P, :, :, :], o[:, :, :, 0:HD], rec, ALU.mult).then_inc(s_on, 1)

            def residual(row):
                dve.wait_ge(s_prj, row.count())
                dve.wait_ge(s_hres, row.count())
                if row.after(1):
                    dve.wait_ge(s_hst, row.plus(-1).count())
                dve.tensor_tensor(h2[0:P, :], ps_tail[0:P, 0:NT * D], h_res[0:P, row.u, :], ALU.add).then_inc(s_h2, 1)
                dve.wait_ge(s_h2, row.count())
                stats(row, h2, st2, s_st2)

            def router_out(row):
                dve.wait_ge(s_sg, row.count())
                dve.tensor_copy(sg_all[0:P, row.index, :, :].rearrange("p t e -> p (t e)"),
                                ps_tail[0:P, 0:NT * (1 + E)]).then_inc(s_sgo, 1)

            dve.wait_ge(s_prep, 2)
            smooth(0, None)

            def iteration(i):
                new, mid, old = i.plus(2), i.plus(1), i.plus(-1)
                for h in range(NH):
                    if h == 1 and old.exists:
                        o_normed(old)
                    if h == 1 and new.exists:
                        dve.wait_ge(s_hin, new.count())
                        stats(new, h_in, st1, s_st1)
                    if h < 4 and mid.exists:
                        score_max(mid, 2 * h)
                    if h == 1 and new.exists:
                        aggregate(new, st1, mv1, ve1, s_ag1, s_ve1)
                    if h < 4 and mid.exists:
                        score_max(mid, 2 * h + 1)
                    if h == 1 and new.exists:
                        normed(new, h_in, mv1, rs1, xn1, s_rs1, s_xn1)
                    if h == 2 and new.exists:
                        low(new, x1l[:], ps_in[:, 0:T], x1h[:], s_x1h, s_x1l)
                    if h == 2 and old.exists:
                        low(old, otl[:], ps_tail[:, 0:T], oth[:], s_oth, s_otl)
                    if h == 4 and mid.exists:
                        max_parts(mid)
                    if h == 3 and old.exists:
                        residual(old)
                    if h == 3 and new.exists:
                        low(new, parts[:, new.u % 2, 0:4:3, :], ps_qk[:, 0:2 * T].rearrange("p (a t) -> p a t", a=2),
                            parts[:, new.u % 2, 1:3, :], s_qkh, s_qkl)
                    if h == 3 and old.exists:
                        aggregate(old, st2, mv2, ve2, s_ag2, s_ve2)
                    if h == 5 and old.exists:
                        normed(old, h2, mv2, rs2, xn2, s_rs2, s_xn2)
                    if h == 6 and old.exists:
                        if old.after(1):
                            dve.wait_ge(s_xst, old.plus(-1).count())
                        low(old, x2l[:], ps_tail[:, 0:T], x2h[:], s_x2h, s_x2l)
                    if h == 7 and old.exists:
                        router_out(old)
                    if h == 7 and new.exists and new.u == U - 1 and (not new.static or new.first + U < B):
                        smooth(new.first // U + 1, new)

            run_pipeline(dve, iteration)

        @block.tensor
        def _(pe):
            pe.wait_ge(s_w, 16 * 9)
            pe.matmul(ps_in[:, 0:D], w_ve4[:], w_linT[:], start=True, stop=True)
            pe.wait_ge(s_wv, 8)
            pe.matmul(ps_in[:, D:2 * D], b_ve_wide[:], w_linT[:], start=True, stop=True).then_inc(s_pw, 1)
            pe.wait_ge(s_pw, 3)
            pe.wait_ge(s_keep, 2 + 2 * RING)

            def three(dst, lhs, rhs, done=None):
                (ah, al), (bh, bl) = lhs, rhs
                pe.matmul(dst, ah, bh, start=True, stop=False)
                pe.matmul(dst, ah, bl, start=False, stop=False)
                return pe.matmul(dst, al, bh, start=False, stop=True)

            def embed(row):
                if row.u == 0:
                    pe.wait_ge(s_smooth, row.first // U + 1)
                if row.after(1):
                    pe.wait_ge(s_vsb, row.plus(-1).count())
                q = row.u * C
                for t in range(NT):
                    last = pe.matmul(ps_in[0:P, t * D:(t + 1) * D], x_smooth[q:q + C, t * P:(t + 1) * P],
                                     w_emb[q:q + C, :], start=True, stop=True)
                last.then_inc(s_emb, 1)

            def turn(row, dst, src, s_in, each, s_done):
                pe.wait_ge(s_in, row.count(each))
                for t in range(NT):
                    last = pe.transpose(dst[:, t * P:(t + 1) * P], src[0:P, t, :], identf[0:P, 0:P])
                last.then_inc(s_done, 1)

            def qk(row):
                pe.wait_ge(s_x1l, row.count())
                if row.after(1):
                    pe.wait_ge(s_qkl, row.plus(-1).count())
                for a in range(2):
                    last = three(ps_qk[:, a * T:(a + 1) * T], (wh[:, a, :], wl[:, a, :]), (x1h[:], x1l[:]))
                last.then_inc(s_qk, 1)

            def values(row):
                pe.wait_ge(s_x1l, row.count())
                for t in range(NT):
                    cols = slice(t * P, (t + 1) * P)
                    last = three(ps_in[0:P, t * D:(t + 1) * D], (x1h[:, cols], x1l[:, cols]), (wh[:, 2, :], wl[:, 2, :]))
                last.then_inc(s_v, 1)

            def scores(row, h):
                if h == 0:
                    pe.wait_ge(s_stack[row.u], dma_count(row, STACK_DMAS))
                if h >= 2 or row.after(1):
                    pe.wait_ge(s_max, row.count(NH, h - 1))
                for t in range(NT):
                    last = pe.matmul(ps_s[h % 2][0:P, t * T:(t + 1) * T], head(0, row, h, ROWS_DOT, t * P, P),
                                     head(1, row, h, ROWS_DOT, 0, T), start=True, stop=True)
                last.then_inc(s_s, 1)

            def turn_max(row):
                pe.wait_ge(s_ml, row.count())
                if row.after(2):
                    pe.wait_ge(s_h2, row.plus(-2).count())
                pe.transpose(ps_max[0:4 * NH, 0:P], mxp[0:P, :, :, :].rearrange("p a b h -> p (a b h)"),
                             identb[0:P, 0:P]).then_inc(s_mt, 1)

            def scores_t(row, h):
                if h == 0:
                    pe.wait_ge(s_mrow[row.u], dma_count(row, 2))
                if h >= 2 or row.after(1):
                    pe.wait_ge(s_exp, row.count(NH, h - 1))
                for t in range(NT):
                    dst = ps_st[h % 2][0:P, t * T:(t + 1) * T]
                    pe.matmul(dst, head(1, row, h, ROWS_ALL, t * P, P), head(0, row, h, ROWS_ALL, 0, T),
                              start=True, stop=True)
                    last = pe.matmul(dst[:, t * P:(t + 1) * P], identb[0:P, 0:P], diag[0:P, t, :],
                                     start=False, stop=True, skip_group_check=True)
                last.then_inc(s_st, 1)

            def weigh(row, h):
                pe.wait_ge(s_exp, row.count(NH, h + 1))
                if h == 0:
                    pe.wait_ge(s_vsb, row.count())
                    if row.after(1):
                        pe.wait_ge(s_on, row.plus(-1).count())
                for t in range(NT):
                    dst = ps_o[0:P, (t * NH + h) * VW:(t * NH + h + 1) * VW]
                    for k in range(NT):
                        last = pe.matmul(dst, pt[0:P, h % RING, k, t * P:(t + 1) * P], v_sb[0:P, row.u, k, h, :],
                                         start=(k == 0), stop=(k == NT - 1))
                last.then_inc(s_pvp, 1)

            def turn_o(row):
                if row.after(1):
                    pe.wait_ge(s_sgo, row.plus(-1).count())
                pe.wait_ge(s_on, row.count())
                for t in range(NT):
                    last = pe.transpose(ps_tail[:, t * P:(t + 1) * P],
                                        o_n[0:P, t, :, :].rearrange("p h d -> p (h d)"), identf[0:P, 0:P])
                last.then_inc(s_ot, 1)

            def project(row):
                pe.wait_ge(s_otl, row.count())
                for t in range(NT):
                    cols = slice(t * P, (t + 1) * P)
                    last = three(ps_tail[0:P, t * D:(t + 1) * D], (oth[:, cols], otl[:, cols]), (wh[:, 3, :], wl[:, 3, :]))
                last.then_inc(s_prj, 1)

            def turn_norm2(row):
                if row.plus(2).exists:
                    pe.wait_ge(s_mrow_made, row.plus(2).count())
                turn(row, ps_tail, xn2, s_xn2, NT, s_x2t)

            def router(row):
                pe.wait_ge(s_x2l, row.count())
                for t in range(NT):
                    cols = slice(t * P, (t + 1) * P)
                    last = three(ps_tail[0:P, t * (1 + E):(t + 1) * (1 + E)], (x2h[:, cols], x2l[:, cols]), (wrh[:], wrl[:]))
                last.then_inc(s_sg, 1)

            def iteration(i):
                new, mid, old = i.plus(2), i.plus(1), i.plus(-1)
                if new.exists:
                    embed(new)
                for h in range(NH):
                    if i.exists:
                        scores_t(i, h)
                    if h < 4 and mid.exists:
                        scores(mid, 2 * h)
                    if h == 0 and old.exists:
                        weigh(old, NH - 1)
                    if h > 0 and i.exists:
                        weigh(i, h - 1)
                    if h < 4 and mid.exists:
                        scores(mid, 2 * h + 1)
                    if h == 2 and new.exists:
                        turn(new, ps_in, xn1, s_xn1, NT, s_x1t)
                    if h == 2 and old.exists:
                        turn_o(old)
                    if h == 3 and new.exists:
                        qk(new)
                    if h == 3 and old.exists:
                        project(old)
                    if h == 5 and mid.exists:
                        turn_max(mid)
                    if h == 5 and new.exists:
                        values(new)
                    if h == 6 and old.exists:
                        turn_norm2(old)
                    if h == 7 and old.exists:
                        router(old)

            run_pipeline(pe, iteration)


def experts_phase(nc, h_all, xt_all, sg_all, consts, attn_b, gate_b, w1, b1, w2, b2, out):
    with ExitStack() as ctx:
        def sb(name, shape, dt=F32):
            return ctx.enter_context(nc.sbuf_tensor(name, shape, dt))

        def sem(name):
            return ctx.enter_context(nc.semaphore(name))

        def bank(name):
            return ctx.enter_context(nc.psum_tensor(name, [D, 512], F32))

        ps_h = [bank(f"ps_h{i}") for i in range(4)]
        ps_e = [bank(f"ps_e{i}") for i in range(2)]
        ps_y = bank("ps_y")
        ps_r = bank("ps_r")

        const = sb("const2", [D, D])
        identf = const[:]
        w1s = sb("w1s", [D, E, 2, HID], BF16)
        w2s = sb("w2s", [D, E, 2, HC, D], BF16)
        w1f = sb("w1f", [D, 2, HID])
        w2f = sb("w2f", [D, 2, HC, D])
        b1f = sb("b1f", [E, HID])
        b2f = sb("b2f", [E, D])
        attn_b_col = sb("attn_b_col", [B, 1])
        gate_b_row = sb("gate_b_row", [B, E])
        ones = sb("ones", [D, D])
        iota = sb("iota", [B, E])
        tok = sb("tok", [B, T])
        tok_e = sb("tok_e", [B, T])
        tok_w = sb("tok_w", [B, T])
        small = sb("small", [B, 16])
        tok_wt = sb("tok_wt", [D, NT, B])
        pooled = sb("pooled", [D, NT, B, E])
        logit = sb("logit", [B, E])
        gate_e = sb("gate_e", [B, E])
        gate = sb("gate", [B, E])
        top = sb("top", [B, 8])
        top_i = sb("top_i", [B, 8], U32)
        top_f = sb("top_f", [B, TOPK])
        weight = sb("weight", [B, TOPK])
        spread = sb("spread", [B, TOPK, B])
        onehot = sb("onehot", [B, TOPK, E])
        onehot_t = sb("onehot_t", [E, TOPK * B])
        chosen = sb("chosen", [1, B * TOPK], U32)
        weight_bc = sb("weight_bc", [D, TOPK, B])
        b1_sel = sb("b1_sel", [D, HC, TOPK, B])
        b2_sel = sb("b2_sel", [D, TOPK, B])
        hid = sb("hid", [D, TOPK, HC, T])
        hid_h = sb("hid_h", [D, TOPK, HC, T], BF16)
        hid_l = sb("hid_l", [D, TOPK, HC, T], BF16)
        eo = sb("eo", [D, TOPK, T])
        y0 = sb("y0", [D, T])
        y = sb("y", [D, T])
        o_sb = sb("o_sb", [D, NT * D])

        s_c, s_cast = sem("router_constants"), sem("experts_split")
        s_w = [sem(f"expert_weights{i}") for i in range(2)]
        s_wh, s_cast_ones, s_oh = sem("expert_hi"), sem("router_fills"), sem("choice_spread")
        s_r, s_rv, s_ra, s_idx = sem("router_pe"), sem("router_dve"), sem("router_act"), sem("chosen_ready")
        s_h, s_hid, s_hh, s_hl = sem("hidden"), sem("hidden_gelu"), sem("hidden_hi"), sem("hidden_lo")
        s_e, s_eo, s_y, s_yt, s_o, s_w_out = (sem(n) for n in (
            "expert_out", "expert_gelu", "weighted", "weighted_turned", "out_ready", "out_written"))
        block = ctx.enter_context(nc.Block())

        @block.sync
        def _(sp):
            sp.dma_start(const[:], consts[:, 0:D]).then_inc(s_c, 16)
            sp.dma_start(attn_b_col[:], attn_b.partition_broadcast(B)).then_inc(s_c, 16)
            sp.dma_start(gate_b_row[:], gate_b.partition_broadcast(B)).then_inc(s_c, 16)
            sp.dma_start(b1f[:], b1).then_inc(s_c, 16)
            sp.dma_start(b2f[:], b2).then_inc(s_c, 16)
            for e in range(E):
                if e >= 2:
                    sp.wait_ge(s_cast, 2 * (e - 1))
                sp.dma_start(w1f[:, e % 2, :], w1[e]).then_inc(s_w[e % 2], 16)
                sp.dma_start(w2f[:, e % 2, :, :], w2[e].rearrange("(c p) o -> p c o", p=D)).then_inc(s_w[e % 2], 16)
            sp.wait_ge(s_rv, 16)
            sp.dma_start(chosen[:], top_i[:, 0:TOPK]).then_inc(s_idx, 16)
            with sp.Fori(0, B, 1) as b:
                sp.wait_ge(s_o, b + 1)
                sp.dma_start(out[b].rearrange("(t p) d -> p t d", p=P),
                             o_sb[0:P, :].rearrange("p (t d) -> p t d", t=NT)).then_inc(s_w_out, 16)
            sp.wait_ge(s_w_out, 16 * B)

        @block.gpsimd
        def _(pool):
            pool.memset(ones[:], 1.0).then_inc(s_cast_ones, 1)
            for e in range(E):
                pool.memset(iota[:, e:e + 1], float(e))
            pool.memset(small[:, 8:9], 0.0).then_inc(s_cast_ones, 1)

        @block.scalar
        def _(act):
            act.wait_ge(s_rv, 2)
            act.activation(tok_e[:], tok[:], ACT.Exp, bias=small[:, 0:1], accum_out=small[:, 1:2]).then_inc(s_ra, 1)
            act.wait_ge(s_rv, 9)
            act.activation(gate_e[:], logit[:], ACT.Exp, bias=small[:, 3:4], accum_out=small[:, 4:5]).then_inc(s_ra, 1)

            def hidden(b, k, s):
                if not isinstance(b, int) or b > 0:
                    act.wait_ge(s_hl, s - 1)
                for half in range(2):
                    act.wait_ge(s_h, s * 2 + half + 1)
                    for j in range(2):
                        c = 2 * half + j
                        last = act.activation(hid[:, k, c, :], ps_h[2 * k + half][:, j * T:(j + 1) * T], ACT.Gelu,
                                              bias=b1_sel[:, c, k, at(b)])
                    last.then_inc(s_hid, 1)

            def output(b, k, s):
                act.wait_ge(s_e, s + 1)
                if not isinstance(b, int) or b > 0:
                    act.wait_ge(s_y, s - 1)
                act.activation(eo[:, k, :], ps_e[k][:, 0:T], ACT.Gelu, bias=b2_sel[:, k, at(b)]).then_inc(s_eo, 1)

            act.wait_ge(s_rv, 19)
            run_steps(act, hidden, output)

        @block.vector
        def _(dve):
            def split(e):
                dve.wait_ge(s_w[e % 2], 32 * (e // 2 + 1))
                dve.tensor_copy(w1s[:, e, 0, :], w1f[:, e % 2, :]).then_inc(s_wh, 1)
                dve.tensor_copy(w2s[:, e, 0, :, :], w2f[:, e % 2, :, :]).then_inc(s_wh, 1)
                dve.wait_ge(s_wh, 2 * (e + 1))
                dve.tensor_tensor(w1s[:, e, 1, :], w1f[:, e % 2, :], w1s[:, e, 0, :], ALU.subtract).then_inc(s_cast, 1)
                dve.tensor_tensor(w2s[:, e, 1, :, :], w2f[:, e % 2, :, :], w2s[:, e, 0, :, :],
                                  ALU.subtract).then_inc(s_cast, 1)

            dve.wait_ge(s_c, 16 * 5)
            dve.wait_ge(s_cast_ones, 2)
            dve.wait_ge(s_r, 1)
            dve.tensor_scalar(tok[:], ps_r[0:B, 0:T], attn_b_col[:, 0:1], None, ALU.add).then_inc(s_rv, 1)
            dve.wait_ge(s_rv, 1)
            dve.tensor_reduce(small[:, 0:1], tok[:], AX_X, ALU.max, negate=True).then_inc(s_rv, 1)
            split(0)
            split(1)
            dve.wait_ge(s_ra, 1)
            dve.reciprocal(small[:, 2:3], small[:, 1:2]).then_inc(s_rv, 1)
            dve.wait_ge(s_rv, 3)
            dve.tensor_scalar(tok_w[:], tok_e[:], small[:, 2:3], None, ALU.mult).then_inc(s_rv, 1)
            dve.wait_ge(s_r, 2)
            dve.tensor_copy(tok_wt[0:P, :, :], ps_y[0:P, 0:NT * B].rearrange("p (t b) -> p t b", t=NT)).then_inc(s_rv, 1)
            dve.wait_ge(s_rv, 5)
            for t in range(NT):
                wide = tok_wt[0:P, t, :].rearrange("p (b o) -> p b o", o=1).broadcast_to([P, B, E])
                dve.tensor_tensor(pooled[0:P, t, :, :], sg_all[0:P, :, t, 1:1 + E], wide, ALU.mult).then_inc(s_rv, 1)
            dve.wait_ge(s_r, 3)
            dve.tensor_tensor(logit[:], ps_r[0:B, 256:256 + E], gate_b_row[:], ALU.add).then_inc(s_rv, 1)
            dve.wait_ge(s_rv, 8)
            dve.tensor_reduce(small[:, 3:4], logit[:], AX_X, ALU.max, negate=True).then_inc(s_rv, 1)
            dve.wait_ge(s_ra, 2)
            dve.reciprocal(small[:, 5:6], small[:, 4:5]).then_inc(s_rv, 1)
            dve.wait_ge(s_rv, 10)
            dve.tensor_scalar(gate[:], gate_e[:], small[:, 5:6], None, ALU.mult).then_inc(s_rv, 1)
            dve.wait_ge(s_rv, 11)
            dve.max(top[:], gate[:]).then_inc(s_rv, 1)
            dve.wait_ge(s_rv, 12)
            dve.max_index(top_i[:], top[:], gate[:]).then_inc(s_rv, 1)
            dve.tensor_reduce(small[:, 6:7], top[:, 0:TOPK], AX_X, ALU.add).then_inc(s_rv, 1)
            dve.wait_ge(s_rv, 14)
            dve.tensor_scalar(small[:, 7:8], small[:, 6:7], 1e-9, None, ALU.add).then_inc(s_rv, 1)
            dve.tensor_copy(top_f[:], top_i[:, 0:TOPK]).then_inc(s_rv, 1)
            dve.wait_ge(s_rv, 16)
            dve.reciprocal(small[:, 9:10], small[:, 7:8]).then_inc(s_rv, 1)
            for k in range(TOPK):
                last = dve.tensor_scalar(onehot[:, k, :], iota[:], top_f[:, k:k + 1], None, ALU.is_equal)
            last.then_inc(s_oh, 1)
            dve.wait_ge(s_rv, 17)
            dve.tensor_scalar(weight[:], top[:, 0:TOPK], small[:, 9:10], None, ALU.mult).then_inc(s_oh, 1)
            dve.wait_ge(s_oh, 2)
            for k in range(TOPK):
                last = dve.tensor_scalar(spread[:, k, :], identf[0:B, 0:B], weight[:, k:k + 1], None, ALU.mult)
            last.then_inc(s_oh, 1)
            dve.wait_ge(s_r, 4)
            dve.tensor_copy(onehot_t[:], ps_y[0:E, 0:TOPK * B]).then_inc(s_oh, 1)
            dve.wait_ge(s_r, 5)
            dve.tensor_copy(weight_bc[:].rearrange("p k b -> p (k b)"), ps_r[:, 0:TOPK * B]).then_inc(s_oh, 1)
            dve.wait_ge(s_r, 6)
            dve.tensor_copy(b1_sel[:].rearrange("p c k b -> p (c k b)"), ps_y[:, 0:HC * TOPK * B]).then_inc(s_rv, 1)
            dve.tensor_copy(b2_sel[:].rearrange("p k b -> p (k b)"), ps_r[:, 128:128 + TOPK * B]).then_inc(s_rv, 1)
            for e in range(2, E):
                split(e)

            def hidden(b, k, s):
                dve.wait_ge(s_hid, s * 2 + 2)
                if not isinstance(b, int) or b > 0:
                    dve.wait_ge(s_e, s - 1)
                dve.tensor_copy(hid_h[:, k, :, :], hid[:, k, :, :]).then_inc(s_hh, 1)
                dve.wait_ge(s_hh, s + 1)
                dve.tensor_tensor(hid_l[:, k, :, :], hid[:, k, :, :], hid_h[:, k, :, :], ALU.subtract).then_inc(s_hl, 1)

            def output(b, k, s):
                dve.wait_ge(s_eo, s + 1)
                if k == 0:
                    dve.tensor_scalar(y0[:], eo[:, 0, :], weight_bc[:, 0, at(b)], None, ALU.mult).then_inc(s_y, 1)
                    return
                dve.wait_ge(s_y, s)
                if not isinstance(b, int) or b > 0:
                    dve.wait_ge(s_yt, b)
                dve.scalar_tensor_tensor(y[:], eo[:, 1, :], weight_bc[:, 1, at(b)], y0[:], ALU.mult,
                                         ALU.add).then_inc(s_y, 1)

            def finish(b):
                dve.wait_ge(s_yt, b + 1)
                if not isinstance(b, int) or b > 0:
                    dve.wait_ge(s_w_out, 16 * b)
                dve.tensor_tensor(o_sb[0:P, :], ps_y[0:P, 0:NT * D], h_all[0:P, b, :], ALU.add).then_inc(s_o, 1)

            run_steps(dve, hidden, output, finish)

        @block.tensor
        def _(pe):
            pe.wait_ge(s_c, 16 * 5)
            pe.wait_ge(s_cast_ones, 2)
            for t in range(NT):
                last = pe.transpose(ps_r[0:B, t * P:(t + 1) * P], sg_all[0:P, :, t, 0], identf[0:P, 0:P])
            last.then_inc(s_r, 1)
            pe.wait_ge(s_rv, 4)
            for t in range(NT):
                last = pe.transpose(ps_y[0:P, t * B:(t + 1) * B], tok_w[:, t * P:(t + 1) * P], identf[0:B, 0:B])
            last.then_inc(s_r, 1)
            pe.wait_ge(s_rv, 7)
            for e in range(E):
                for t in range(NT):
                    last = pe.matmul(ps_r[0:B, 256 + e:257 + e], pooled[0:P, t, :, e], ones[0:P, 0:1],
                                     start=(t == 0), stop=(t == NT - 1))
            last.then_inc(s_r, 1)
            pe.wait_ge(s_oh, 1)
            for k in range(TOPK):
                last = pe.transpose(ps_y[0:E, k * B:(k + 1) * B], onehot[:, k, :], identf[0:B, 0:B])
            last.then_inc(s_r, 1)
            pe.wait_ge(s_oh, 3)
            for k in range(TOPK):
                last = pe.matmul(ps_r[:, k * B:(k + 1) * B], ones[0:B, :], spread[:, k, :], start=True, stop=True)
            last.then_inc(s_r, 1)
            pe.wait_ge(s_oh, 5)
            for c in range(HC):
                pe.matmul(ps_y[:, c * TOPK * B:(c + 1) * TOPK * B], b1f[:, c * D:(c + 1) * D], onehot_t[:],
                          start=True, stop=True)
            pe.matmul(ps_r[:, 128:128 + TOPK * B], b2f[:], onehot_t[:], start=True, stop=True).then_inc(s_r, 1)
            pe.wait_ge(s_rv, 19)
            pe.wait_ge(s_cast, 2 * E)
            pe.wait_ge(s_idx, 16)

            def hidden(b, k, s):
                e = pe.value_load(chosen[0:1, at(s)], min_val=0, max_val=E - 1)
                if not isinstance(b, int) or b > 0:
                    pe.wait_ge(s_hid, s * 2 - 2)
                for half in range(2):
                    for j in range(2):
                        c = 2 * half + j
                        dst = ps_h[2 * k + half][:, j * T:(j + 1) * T]
                        for n, (wp, xp) in enumerate(((0, 0), (0, 1), (1, 0))):
                            last = pe.matmul(dst, w1s[:, e, wp, c * D:(c + 1) * D], xt_all[:, b, xp, :],
                                             start=(n == 0), stop=(n == 2))
                    last.then_inc(s_h, 1)

            def output(b, k, s):
                e = pe.value_load(chosen[0:1, at(s)], min_val=0, max_val=E - 1)
                pe.wait_ge(s_hl, s + 1)
                if not isinstance(b, int) or b > 0:
                    pe.wait_ge(s_eo, s - 1)
                for c in range(HC):
                    for n, (wp, part) in enumerate(((0, hid_h), (0, hid_l), (1, hid_h))):
                        last = pe.matmul(ps_e[k][:, 0:T], w2s[:, e, wp, c, :], part[:, k, c, :],
                                         start=(c == 0 and n == 0), stop=(c == HC - 1 and n == 2))
                last.then_inc(s_e, 1)

            def finish(b):
                pe.wait_ge(s_y, b * 2 + 2)
                if not isinstance(b, int) or b > 0:
                    pe.wait_ge(s_o, b)
                for t in range(NT):
                    last = pe.transpose(ps_y[0:P, t * D:(t + 1) * D], y[:, t * P:(t + 1) * P], identf)
                last.then_inc(s_yt, 1)

            run_steps(pe, hidden, output, finish)


def at(i):
    return slice(i, i + 1) if isinstance(i, int) else bass.ds(i, 1)


def run_steps(eng, hidden, output, finish=None):
    def row(b, first=False, last=False):
        hidden(b, 1, b * 2 + 1)
        output(b, 0, b * 2)
        if finish is not None and not first:
            finish(b - 1)
        if not last:
            hidden(b + 1, 0, b * 2 + 2)
        output(b, 1, b * 2 + 1)

    hidden(0, 0, 0)
    row(0, first=True)
    with eng.Fori(1, B - 1, 1) as b:
        row(b)
    row(B - 1, last=True)
    if finish is not None:
        finish(B - 1)


def bass_audio_tower(nc, consts, x, W_ve, W_lin_T, b_ve, b_lin, w_qkv_T, w_out_T, b_out,
                     attn_w, attn_b, gate_w, gate_b, w1, b1, w2, b2, out):
    with ExitStack() as ctx:
        h_all = ctx.enter_context(nc.sbuf_tensor("h_all", [D, B, NT * D], F32))
        xt_all = ctx.enter_context(nc.sbuf_tensor("xt_all", [D, B, 2, T], BF16))
        sg_all = ctx.enter_context(nc.sbuf_tensor("sg_all", [D, B, NT, 1 + E], F32))
        attention_phase(nc, h_all, xt_all, sg_all, consts, x, W_ve, W_lin_T, b_ve, b_lin, w_qkv_T,
                        w_out_T, b_out, attn_w, gate_w)
        experts_phase(nc, h_all, xt_all, sg_all, consts, attn_b, gate_b, w1, b1, w2, b2, out)


_INS = ["x", "W_ve", "W_lin_T", "b_ve", "b_lin", "w_qkv_T", "w_out_T", "b_out", "attn_w", "attn_b",
        "gate_w", "gate_b", "w1", "b1", "w2", "b2"]


def kernel(x, L0_tok_W_ve, L0_tok_b_ve, L0_tok_W_lin, L0_tok_b_lin, L0_attn_w_qkv, L0_attn_w_out,
           L0_attn_b_out, L0_ffn_attn_w, L0_ffn_attn_b, L0_ffn_gate_w, L0_ffn_gate_b, L0_ffn_w1,
           L0_ffn_b1, L0_ffn_w2, L0_ffn_b2):
    import concourse.bacc as bacc
    from concourse.bass_utils import run_bass_kernel_spmd

    qkv = np.asarray(L0_attn_w_qkv)
    qk = qkv[:2 * D].reshape(2, NH // 2, 2, HD, D).transpose(0, 2, 3, 1, 4).reshape(2 * D, D)
    qkv_T = np.concatenate([qk, qkv[2 * D:]]).T

    laid_out = {
        "consts": constants(), "x": x, "W_ve": L0_tok_W_ve, "W_lin_T": np.asarray(L0_tok_W_lin).T,
        "b_ve": L0_tok_b_ve, "b_lin": L0_tok_b_lin, "w_qkv_T": qkv_T,
        "w_out_T": np.asarray(L0_attn_w_out).T, "b_out": L0_attn_b_out, "attn_w": L0_ffn_attn_w,
        "attn_b": L0_ffn_attn_b, "gate_w": L0_ffn_gate_w, "gate_b": L0_ffn_gate_b, "w1": L0_ffn_w1,
        "b1": L0_ffn_b1, "w2": L0_ffn_w2, "b2": L0_ffn_b2,
    }
    nc = bacc.Bacc("TRN2", target_bir_lowering=False, num_devices=1)
    arrays, args = {}, []
    for name, a in laid_out.items():
        a = np.ascontiguousarray(a)
        arrays[f"in_{name}"] = a
        args.append(nc.dram_tensor(f"in_{name}", a.shape, mybir.dt.from_np(a.dtype), kind="ExternalInput").ap())
    args.append(nc.dram_tensor("out_h", (B, T, D), F32, kind="ExternalOutput").ap())
    bass_audio_tower(nc, *args)
    got = run_bass_kernel_spmd(nc, [arrays], core_ids=[0])
    return got.results[0]["out_h"]
```

```python
import math
from contextlib import ExitStack

import numpy as np

import concourse.bass as bass
from concourse import mybir

F32 = mybir.dt.float32
BF16 = mybir.dt.bfloat16
U32 = mybir.dt.uint32
ALU = mybir.AluOpType
ACT = mybir.ActivationFunctionType
AX_X = mybir.AxisListType.X

B, C, T = 64, 32, 250
D = 128
NH, HD = 8, 16
E, HID, TOPK = 8, 512, 2
P = 125
NT = T // P
U = 4
G = B // U
HC = HID // D
VW = HD + 1
RING = 4

ALPHA = 0.1
LAMBDA = -math.log(0.9)
Q_SCALE = 1.0 / (math.sqrt(HD) * LAMBDA)
EPS = 1e-5

ROWS_DOT, ROWS_MAX = 3 * HD, 96
ROW_K, ROW_1, ROW_M = ROWS_MAX, ROWS_MAX + 1, ROWS_MAX + 2
ROWS_ALL = ROWS_MAX + 4
HG = 4
CG = D // HG

def constants():
    k = np.arange(P)[:, None]
    q = np.arange(P)[None, :]
    ident = np.eye(D, dtype=np.float32)
    diag = np.zeros((D, NT, P), np.float32)
    diag[:P, 0] = np.maximum(k - q, 0)
    diag[:P, 1] = np.maximum(q - k, 0)
    qrows = np.zeros((D, T), np.float32)
    krows = np.zeros((D, T), np.float32)
    krows[ROW_K, :P] = -np.arange(P)
    qrows[ROW_K] = 1
    krows[ROW_1, :P] = 1
    qrows[ROW_1] = np.arange(T)
    krows[ROW_M:ROW_M + 2] = -1
    return np.ascontiguousarray(np.concatenate([ident, diag.reshape(D, -1), qrows, krows], axis=1))


class Row:

    def __init__(self, first, u):
        self.first, self.u = first, u

    def plus(self, k):
        carry, u = divmod(self.u + k, U)
        return Row(self.first + U * carry if carry else self.first, u)

    @property
    def static(self):
        return isinstance(self.first, int)

    def count(self, each=1, upto=None):
        upto = each if upto is None else upto
        return self.first * each + (self.u * each + upto)

    @property
    def index(self):
        return self.first + self.u if self.u or self.static else self.first

    @property
    def exists(self):
        return not self.static or 0 <= self.first + self.u < B

    def after(self, k):
        return not self.static or self.first + self.u - k >= 0


def run_pipeline(eng, iteration):
    for i in range(-4, U):
        iteration(Row(0, 0).plus(i))
    with eng.Fori(U, B - 2 * U, U) as first:
        for u in range(U):
            iteration(Row(first, u))
    for i in range(B - 2 * U, B + 2):
        iteration(Row(0, 0).plus(i))


def dma_count(row, each):
    return 16 * each * (row.first // U + 1) if row.static else row.first * (16 * each // U) + 16 * each


def smooths_next(row):
    return row.exists and row.u == U - 1 and (not row.static or row.first + U < B)


def attention_phase(nc, h_all, xt_all, sg_all, consts, x, W_ve, W_lin_T, b_ve, b_lin, w_qkv_T,
                    w_out_T, b_out, attn_w, gate_w):
    with ExitStack() as ctx:
        def sb(name, shape, dt=F32):
            return ctx.enter_context(nc.sbuf_tensor(name, shape, dt))

        def sem(name):
            return ctx.enter_context(nc.semaphore(name))

        def bank(name):
            return ctx.enter_context(nc.psum_tensor(name, [D, 512], F32))

        ps_s = [bank(f"ps_s{i}") for i in range(2)]
        ps_st = [bank(f"ps_st{i}") for i in range(2)]
        ps_in = bank("ps_in")
        ps_qk = bank("ps_qk")
        ps_o = bank("ps_o")
        ps_tail = bank("ps_tail")
        ps_max = ps_tail[:, 0:P].bitcast(BF16)[:, 0:P]

        identf = sb("identf", [D, D])
        identb = sb("identb", [D, D], BF16)
        diag = sb("diag", [D, NT, P], BF16)
        stacks = sb("stacks", [D, RING, 2, NH, T], BF16)
        x_raw = sb("x_raw", [D, T])
        x_diff = sb("x_diff", [D, T])
        x_left = sb("x_left", [D, T])
        x_sum = sb("x_sum", [D, T])
        keep = sb("keep", [D, 1])
        starts = sb("starts", [D, 2])
        w_emb = sb("w_emb", [D, U, D])
        bias_in = sb("bias_in", [D, D])
        b_out_row = sb("b_out_row", [D, D])
        w_att = sb("w_att", [D, 4, D])
        wrf = sb("wrf", [D, 1 + E])
        wrh = sb("wrh", [D, 1 + E], BF16)
        wrl = sb("wrl", [D, 1 + E], BF16)
        power = sb("power", [D, NT])
        h_raw = sb("h_raw", [D, NT, D])
        h_in = sb("h_in", [D, NT, D])
        st1, st2 = sb("st1", [D, NT, 6]), sb("st2", [D, NT, 6])
        mv1, mv2 = sb("mv1", [D, NT, 2]), sb("mv2", [D, NT, 2])
        ve1, ve2 = sb("ve1", [D, 2, NT]), sb("ve2", [D, 2, NT])
        rs1, rs2 = sb("rs1", [D, 2, NT]), sb("rs2", [D, 2, NT])
        xn1, xn2 = sb("xn1", [D, NT, D]), sb("xn2", [D, NT, D])
        x1t = sb("x1t", [D, T])
        parts = sb("parts", [D, 4, T], BF16)
        v_sb = sb("v_sb", [D, RING, NT, NH, VW])
        mx = sb("mx", [D, NH * NT])
        mxp = sb("mxp", [D, 2, NH * NT], BF16)
        mxt = sb("mxt", [2 * NH * NT, P], BF16)
        pt = sb("pt", [D, NH, NT, T])
        o_sb = sb("o_sb", [D, 2, T])
        o_rec = sb("o_rec", [D, NT, NH])
        o_n = sb("o_n", [D, NT, NH, HD])
        ot = o_sb[:, 0, :]

        spare = xt_all[:, B - 8:B, :, :].rearrange("p b a t -> p (b a t)").bitcast(F32)
        const = spare[:, 0:D + NT * P + 2 * T]
        at0 = D + NT * P + 2 * T
        w_linT = spare[:, at0:at0 + D]
        b_ve_wide = spare[:, at0 + D:at0 + 2 * D]
        b_lin_row = spare[:, at0 + 2 * D:at0 + 3 * D]
        w_q_raw = spare[:, at0 + 3 * D:at0 + 4 * D]
        w_ve_wide = spare[:, at0 + 4 * D:at0 + 5 * D]
        b_ve_col = spare[:, at0 + 5 * D:at0 + 5 * D + 1]

        scratch = [nc.dram_tensor(f"scratch{i}", (6, D, T), BF16, kind="Internal").ap() for i in range(2)]

        s_parts = [sem(f"parts_in_dram{i}") for i in range(RING)]
        s_const, s_w, s_x = sem("consts_loaded"), sem("weights_loaded"), sem("x_loaded")
        s_stack = [sem(f"stack_in_place{i}") for i in range(RING)]
        s_mrow = [sem(f"max_rows_in_place{i}") for i in range(RING)]
        s_prep, s_pv, s_pw = sem("prepared_vector"), sem("prepared_pool"), sem("embedding_product")
        s_keep, s_wv = sem("vector_constants"), sem("weights_ready")
        s_diff, s_scan, s_smooth = sem("x_diff_made"), sem("x_scans"), sem("x_smoothed")
        s_ends = sem("x_ends")
        (s_emb, s_hraw, s_hin, s_hres, s_st1, s_ag1, s_ve1, s_rp1, s_rs1, s_xn1, s_x1t, s_x1e, s_qk,
         s_qkh, s_qkl, s_v, s_vsb) = (sem(n) for n in (
            "embedded", "embedding_out", "bias_added", "residual_kept", "stats1", "aggr1", "var1",
            "power1", "rstd1", "norm1", "norm1_turned", "norm1_out", "qk_product", "qk_hi", "qk_lo",
            "v_product", "v_out"))
        (s_s, s_max, s_mh, s_ml, s_mt, s_mr, s_st, s_exp, s_pvp) = (sem(n) for n in (
            "scores", "score_max", "max_hi", "max_lo", "max_turned", "max_rows", "scores_t",
            "exp_done", "pv_product"))
        (s_oev, s_oq, s_rec, s_on, s_ot, s_otb, s_prj, s_h2, s_st2, s_ag2, s_ve2, s_rp2, s_rs2, s_xn2,
         s_x2t, s_x2h, s_x2l, s_sg, s_sgo) = (sem(n) for n in (
            "o_out", "o_by_token", "recip", "o_normed", "o_turned", "o_turned_out", "o_projected",
            "h2_made", "stats2", "aggr2", "var2", "power2", "rstd2", "norm2", "norm2_turned",
            "norm2_hi", "norm2_lo", "router_product", "router_out"))

        def head(which, row, h, rows, lo, n):
            return stacks[0:rows, row.u, which, h, lo:lo + n]

        def x_group(group):
            return x.rearrange("(g q) c t -> g (q c) t", q=U)[group]

        def wide(a, n=NT):
            return a.rearrange("p (o d) -> p o d", o=1).broadcast_to([a.shape[0], n, a.shape[1]])

        block = ctx.enter_context(nc.Block())

        @block.sync
        def _(sp):
            sp.dma_start(const, consts).then_inc(s_const, 16)
            sp.dma_start(identf[:], consts[:, 0:D]).then_inc(s_const, 16)
            sp.dma_start(x_raw[:], x_group(0)).then_inc(s_x, 16)
            sp.dma_start(w_ve_wide.rearrange("p (q c) -> p q c", q=U),
                         W_ve.rearrange("d (o c) -> d o c", o=1).broadcast_to([D, U, C])).then_inc(s_w, 16)
            sp.dma_start(w_linT, W_lin_T).then_inc(s_w, 16)
            sp.dma_start(b_ve_col, b_ve.rearrange("(d o) -> d o", o=1)).then_inc(s_w, 16)
            sp.dma_start(b_lin_row, b_lin.partition_broadcast(D)).then_inc(s_w, 16)
            sp.dma_start(b_out_row[:], b_out.partition_broadcast(D)).then_inc(s_w, 16)
            sp.dma_start(w_q_raw, w_qkv_T[:, 0:D]).then_inc(s_w, 16)
            sp.dma_start(w_att[:, 1:3, :], w_qkv_T[:, D:3 * D].rearrange("p (a d) -> p a d", a=2)).then_inc(s_w, 16)
            sp.dma_start(w_att[:, 3, :], w_out_T).then_inc(s_w, 16)
            sp.dma_start(wrf[:, 0:1], attn_w).then_inc(s_w, 16)
            sp.dma_start(wrf[:, 1:1 + E], gate_w).then_inc(s_w, 16)
            sp.wait_ge(s_keep, 2 + 2 * RING)

            def max_rows(row):
                sp.wait_ge(s_mr, row.count())
                sp.dma_start(stacks[ROW_M:ROW_M + 2, row.u, 0, :, :].rearrange("r h (t p) -> r (h t) p", t=NT),
                             mxt[:]).then_inc(s_mrow[row.u], 16)

            def stack(row):
                sp.wait_ge(s_qkh, row.count())
                sp.wait_ge(s_qkl, row.count())
                place = scratch[row.u % 2]
                for first in range(3):
                    sp.dma_start(place[2 * first:2 * first + 2].rearrange("g p t -> p g t"),
                                 parts[:, first:first + 2, :]).then_inc(s_parts[row.u], 16)
                sp.wait_ge(s_parts[row.u], dma_count(row, 3))
                for which in range(2):
                    src = place[3 * which:3 * which + 3]
                    sp.dma_start(stacks[0:ROWS_DOT, row.u, which, :, :],
                                 src.rearrange("g (d h) t -> g d (h t)", d=HD)).then_inc(s_stack[row.u], 16)

            def iteration(i):
                emb, new, nxt = i.plus(4), i.plus(3), i.plus(1)
                if nxt.exists:
                    max_rows(nxt)
                if new.exists:
                    stack(new)
                if smooths_next(emb):
                    sp.wait_ge(s_diff, emb.first // U + 1)
                    sp.dma_start(x_raw[:], x_group(emb.first // U + 1)).then_inc(s_x, 16)

            run_pipeline(sp, iteration)

        @block.gpsimd
        def _(pool):
            pool.memset(power[:], -0.5).then_inc(s_pv, 1)
            pool.memset(v_sb[:], 1.0).then_inc(s_pv, 1)
            pool.wait_ge(s_pv, 2)
            pool.wait_ge(s_w, 16 * 10)
            pool.wait_ge(s_pw, 2)

            def embed_out(row):
                pool.wait_ge(s_hraw, row.count())
                if row.after(1):
                    pool.wait_ge(s_xn1, row.plus(-1).count(NT))
                    pool.wait_ge(s_hres, row.plus(-1).count())
                pool.tensor_tensor(h_in[0:P, :, :], h_raw[0:P, :, :], wide(bias_in[0:P, :]), ALU.add).then_inc(s_hin, 1)

            def keep_residual(row):
                pool.wait_ge(s_hin, row.count())
                pool.tensor_tensor(h_all[0:P, row.index, :].rearrange("p (t d) -> p t d", t=NT), h_in[0:P, :, :],
                                   wide(b_out_row[0:P, :]), ALU.add).then_inc(s_hres, 1)

            def deviation(row, ve, rs, s_var, s_pow, s_rs):
                pool.wait_ge(s_var, row.count(2))
                pool.tensor_tensor(rs[0:P, 0, :], ve[0:P, 0, :], power[0:P, :], ALU.pow).then_inc(s_pow, 1)
                pool.wait_ge(s_pow, row.count())
                pool.tensor_tensor(rs[0:P, 1, :], ve[0:P, 1, :], rs[0:P, 0, :], ALU.mult).then_inc(s_rs, 1)

            def iteration(i):
                emb, old = i.plus(4), i.plus(-1)
                if emb.exists:
                    embed_out(emb)
                    deviation(emb, ve1, rs1, s_ve1, s_rp1, s_rs1)
                if old.exists:
                    deviation(old, ve2, rs2, s_ve2, s_rp2, s_rs2)
                if emb.exists:
                    keep_residual(emb)

            run_pipeline(pool, iteration)

        @block.scalar
        def _(act):
            act.wait_ge(s_pv, 2)

            def embed_out(row):
                act.wait_ge(s_emb, row.count())
                if row.after(1):
                    act.wait_ge(s_hin, row.plus(-1).count())
                act.copy(h_raw[0:P, :, :].rearrange("p t d -> p (t d)"), ps_in[0:P, 0:NT * D]).then_inc(s_hraw, 1)

            def normed(row, src, rs, xn, s_rs, s_turned, s_done):
                act.wait_ge(s_rs, row.count())
                if row.after(1):
                    act.wait_ge(s_turned, row.plus(-1).count())
                for t in range(NT):
                    act.activation(xn[0:P, t, :], src(t), ACT.Identity, bias=rs[0:P, 1, t:t + 1],
                                   scale=rs[0:P, 0, t:t + 1]).then_inc(s_done, 1)

            def norm1_out(row):
                act.wait_ge(s_x1t, row.count())
                if row.after(1):
                    act.wait_ge(s_v, row.plus(-1).count())
                act.copy(x1t[:], ps_in[:, 0:T]).then_inc(s_x1e, 1)

            def qk_hi(row):
                act.wait_ge(s_qk, row.count())
                if row.after(1):
                    act.wait_ge(s_parts[(row.u - 1) % RING], dma_count(row.plus(-1), 3))
                act.copy(parts[:, 1:3, :], ps_qk[:, 0:2 * T].rearrange("p (a t) -> p a t", a=2)).then_inc(s_qkh, 1)

            def v_out(row):
                act.wait_ge(s_v, row.count())
                act.copy(v_sb[0:P, row.u, :, :, 0:HD],
                         ps_in[0:P, 0:NT * D].rearrange("p (t h d) -> p t h d", t=NT, h=NH)).then_inc(s_vsb, 1)

            def exps(row, h):
                act.wait_ge(s_st, row.count(NH, h + 1))
                if h % HG == 0 and row.after(1):
                    act.wait_ge(s_pvp, row.plus(-1).count(2, h // HG + 1))
                act.activation(pt[0:P, h, :, :].rearrange("p a t -> p (a t)"),
                               ps_st[h % 2][0:P, 0:NT * T], ACT.Exp, scale=LAMBDA).then_inc(s_exp, 1)

            def max_out(row):
                act.wait_ge(s_mt, row.count())
                if row.after(1):
                    act.wait_ge(s_mrow[(row.u - 1) % RING], dma_count(row.plus(-1), 1))
                act.copy(mxt[:], ps_max[0:2 * NH * NT, :]).then_inc(s_mr, 1)

            def o_out(row):
                act.wait_ge(s_pvp, row.count(2))
                if row.after(1):
                    act.wait_ge(s_prj, row.plus(-1).count())
                act.copy(o_sb[:].rearrange("p g t -> p (g t)"), ps_o[:, 0:2 * T]).then_inc(s_oev, 1)

            def o_turned_out(row):
                act.wait_ge(s_ot, row.count())
                act.copy(ot, ps_tail[:, 0:T]).then_inc(s_otb, 1)

            def norm2_hi(row):
                act.wait_ge(s_x2t, row.count())
                act.copy(xt_all[:, row.index, 0, :], ps_tail[:, 0:T]).then_inc(s_x2h, 1)

            def iteration(i):
                emb, new, nxt, old, done = i.plus(4), i.plus(3), i.plus(1), i.plus(-1), i.plus(-2)
                for h in range(NH):
                    if i.exists:
                        exps(i, h)
                    if h == 0 and nxt.exists:
                        max_out(nxt)
                    if h == 0 and new.exists:
                        norm1_out(new)
                    if h == 1 and old.exists:
                        o_out(old)
                    if h == 1 and done.exists:
                        norm2_hi(done)
                    if h == 2 and new.exists:
                        qk_hi(new)
                    if h == 3 and new.exists:
                        v_out(new)
                    if h == 4 and emb.exists:
                        embed_out(emb)
                    if h == 5 and old.exists:
                        o_turned_out(old)
                    if h == 6 and emb.exists:
                        normed(emb, lambda t: h_in[0:P, t, :], rs1, xn1, s_rs1, s_x1t, s_xn1)
                    if h == 7 and old.exists:
                        normed(old, lambda t: h_all[0:P, old.index, t * D:(t + 1) * D], rs2, xn2, s_rs2, s_x2t, s_xn2)

            run_pipeline(act, iteration)

        @block.vector
        def _(dve):
            dve.memset(keep[:], 1.0 - ALPHA).then_inc(s_prep, 1)
            dve.memset(x_diff[:, 0:1], 0.0).then_inc(s_prep, 1)
            dve.memset(w_emb[:], 0.0).then_inc(s_prep, 1)
            dve.memset(ps_o[:], 0.0).then_inc(s_prep, 1)
            dve.wait_ge(s_const, 32)
            dve.tensor_copy(identb[:], identf[:]).then_inc(s_keep, 1)
            dve.tensor_copy(diag[:].rearrange("p a t -> p (a t)"), const[:, D:D + NT * P]).then_inc(s_keep, 1)
            for which in range(2):
                at = D + NT * P + which * T
                for r in range(RING):
                    dve.tensor_copy(stacks[:, r, which, :, :], wide(const[:, at:at + T], NH)).then_inc(s_keep, 1)
            dve.wait_ge(s_w, 16 * 10)
            dve.tensor_scalar(w_att[:, 0, :], w_q_raw, Q_SCALE, None, ALU.mult).then_inc(s_wv, 1)
            dve.tensor_copy(wrh[:], wrf[:]).then_inc(s_wv, 1)
            dve.wait_ge(s_wv, 2)
            dve.tensor_tensor(wrl[:], wrf[:], wrh[:], ALU.subtract).then_inc(s_wv, 1)
            dve.tensor_scalar(b_ve_wide, identf[:], 0.0, b_ve_col, ALU.mult, ALU.add).then_inc(s_wv, 1)
            dve.wait_ge(s_pw, 1)
            dve.wait_ge(s_prep, 4)
            dve.tensor_tensor(bias_in[:], ps_in[:, D:2 * D], b_lin_row, ALU.add).then_inc(s_pw, 1)
            for q in range(U):
                r = slice(q * C, (q + 1) * C)
                dve.tensor_scalar(w_emb[r, q, :], ps_in[r, 0:D], ALPHA / 2, None, ALU.mult).then_inc(s_pw, 1)

            def smooth(group, last_row):
                dve.wait_ge(s_x, group * 16 + 16)
                dve.tensor_tensor(x_diff[:, 1:T], x_raw[:, 1:T], x_raw[:, 0:T - 1], ALU.subtract).then_inc(s_diff, 1)
                dve.wait_ge(s_diff, group + 1)
                dve.tensor_scalar(starts[:], x_diff[:, 0:T:T - 1], 1.0 / ALPHA, None, ALU.mult).then_inc(s_ends, 1)
                dve.wait_ge(s_ends, group * 3 + 1)
                kept = keep[:].broadcast_to([D, T - 1])
                dve.tensor_tensor_scan(x_left[:, 1:T], kept, x_diff[:, 1:T], starts[:, 0:1],
                                       ALU.mult, ALU.add).then_inc(s_scan, 1)
                dve.tensor_copy(x_left[:, 0:1], starts[:, 0:1]).then_inc(s_ends, 1)
                dve.wait_ge(s_scan, group * 2 + 1)
                dve.tensor_tensor_scan(x_diff[:, T - 2::-1], kept, x_diff[:, T - 2::-1], starts[:, 1:2],
                                       ALU.mult, ALU.add).then_inc(s_scan, 1)
                dve.tensor_copy(x_diff[:, T - 1:T], starts[:, 1:2]).then_inc(s_ends, 1)
                dve.wait_ge(s_scan, group * 2 + 2)
                dve.wait_ge(s_ends, group * 3 + 3)
                if last_row is not None:
                    dve.wait_ge(s_emb, last_row.count())
                dve.tensor_tensor(x_sum[:], x_left[:], x_diff[:], ALU.add).then_inc(s_smooth, 1)
                dve.wait_ge(s_smooth, group * 2 + 1)
                dve.memset(x_diff[:, 0:1], 0.0).then_inc(s_smooth, 1)

            def score_max(row, h):
                dve.wait_ge(s_s, row.count(NH, h + 1))
                if h == 0 and row.after(1):
                    dve.wait_ge(s_ml, row.plus(-1).count())
                dve.tensor_reduce(mx[0:P, h * NT:(h + 1) * NT],
                                  ps_s[h % 2][0:P, 0:NT * T].rearrange("p (a t) -> p a t", a=NT),
                                  AX_X, ALU.max).then_inc(s_max, 1)

            def max_parts(row):
                dve.wait_ge(s_max, row.count(NH))
                if row.after(1):
                    dve.wait_ge(s_mt, row.plus(-1).count())
                dve.tensor_copy(mxp[0:P, 0, :], mx[0:P, :]).then_inc(s_mh, 1)
                dve.wait_ge(s_mh, row.count())
                dve.tensor_tensor(mxp[0:P, 1, :], mx[0:P, :], mxp[0:P, 0, :], ALU.subtract).then_inc(s_ml, 1)

            def stats(row, src, st, s_stat):
                for t in range(NT):
                    dve.bn_stats(st[0:P, t, :], src(t)).then_inc(s_stat, 1)

            def aggregate(row, st, mv, ve, s_agg, s_var):
                for t in range(NT):
                    dve.bn_aggr(mv[0:P, t, :], st[0:P, t, :]).then_inc(s_agg, 1)
                dve.wait_ge(s_agg, row.count(NT))
                dve.tensor_scalar(ve[0:P, 0, :], mv[0:P, :, 1], EPS, None, ALU.add).then_inc(s_var, 1)
                dve.tensor_scalar(ve[0:P, 1, :], mv[0:P, :, 0], -1.0, None, ALU.mult).then_inc(s_var, 1)

            def low(row, dst, psum, hi, s_hi, s_lo):
                dve.wait_ge(s_hi, row.count())
                dve.tensor_tensor(dst, psum, hi, ALU.subtract).then_inc(s_lo, 1)

            def o_normed(row):
                dve.wait_ge(s_oq, row.count())
                o = ps_tail[0:P, :].rearrange("p (t h d) -> p t h d", t=NT, h=NH)
                dve.reciprocal(o_rec[0:P, :, :], o[:, :, :, HD]).then_inc(s_rec, 1)
                dve.wait_ge(s_rec, row.count())
                rec = o_rec[0:P, :, :].rearrange("p t (h o) -> p t h o", o=1).broadcast_to([P, NT, NH, HD])
                dve.tensor_tensor(o_n[0:P, :, :, :], o[:, :, :, 0:HD], rec, ALU.mult).then_inc(s_on, 1)

            def residual(row):
                dve.wait_ge(s_prj, row.count())
                dve.wait_ge(s_hres, row.count())
                h = h_all[0:P, row.index, :]
                dve.tensor_tensor(h, ps_tail[0:P, 0:NT * D], h, ALU.add).then_inc(s_h2, 1)

            def router_out(row):
                dve.wait_ge(s_sg, row.count())
                dve.tensor_copy(sg_all[0:P, row.index, :, :].rearrange("p t e -> p (t e)"),
                                ps_tail[0:P, 0:NT * (1 + E)]).then_inc(s_sgo, 1)

            smooth(0, None)

            def iteration(i):
                emb, new, mid, old, done = i.plus(4), i.plus(3), i.plus(2), i.plus(-1), i.plus(-2)
                for h in range(NH):
                    if h == 4 and old.exists:
                        o_normed(old)
                    if h == 5 and emb.exists:
                        dve.wait_ge(s_hin, emb.count())
                        stats(emb, lambda t: h_in[0:P, t, :], st1, s_st1)
                        dve.wait_ge(s_st1, emb.count(NT))
                    if h == 7 and old.exists:
                        dve.wait_ge(s_h2, old.count())
                    if mid.exists:
                        score_max(mid, h)
                    if h == 2 and done.exists:
                        low(done, xt_all[:, done.index, 1, :], ps_tail[:, 0:T], xt_all[:, done.index, 0, :],
                            s_x2h, s_x2l)
                    if h == 2 and new.exists:
                        low(new, parts[:, 0:4:3, :], ps_qk[:, 0:2 * T].rearrange("p (a t) -> p a t", a=2),
                            parts[:, 1:3, :], s_qkh, s_qkl)
                    if h == 3 and done.exists:
                        router_out(done)
                    if h == 5 and emb.exists:
                        aggregate(emb, st1, mv1, ve1, s_ag1, s_ve1)
                    if h == 6 and old.exists:
                        residual(old)
                    if h == 7 and old.exists:
                        stats(old, lambda t: h_all[0:P, old.index, t * D:(t + 1) * D], st2, s_st2)
                        dve.wait_ge(s_st2, old.count(NT))
                    if h == 7 and mid.exists:
                        max_parts(mid)
                    if h == 7 and old.exists:
                        aggregate(old, st2, mv2, ve2, s_ag2, s_ve2)
                    if h == 7 and smooths_next(emb):
                        smooth(emb.first // U + 1, emb)

            run_pipeline(dve, iteration)

        @block.tensor
        def _(pe):
            pe.wait_ge(s_w, 16 * 10)
            pe.matmul(ps_in[:, 0:D], w_ve_wide, w_linT, start=True, stop=True)
            pe.wait_ge(s_wv, 4)
            pe.matmul(ps_in[:, D:2 * D], b_ve_wide, w_linT, start=True, stop=True).then_inc(s_pw, 1)
            pe.wait_ge(s_pw, 2 + U)
            pe.wait_ge(s_keep, 2 + 2 * RING)

            def embed(row):
                if row.u == 0:
                    pe.wait_ge(s_smooth, row.first // U * 2 + 1)
                if row.after(1):
                    pe.wait_ge(s_vsb, row.plus(-1).count())
                for t in range(NT):
                    last = pe.matmul(ps_in[0:P, t * D:(t + 1) * D], x_sum[:, t * P:(t + 1) * P],
                                     w_emb[:, row.u, :], start=True, stop=True)
                last.then_inc(s_emb, 1)

            def turn(dst, src):
                for t in range(NT):
                    last = pe.transpose(dst[:, t * P:(t + 1) * P], src(t), identf[0:P, 0:P])
                return last

            def turn_norm1(row):
                pe.wait_ge(s_xn1, row.count(NT))
                turn(ps_in, lambda t: xn1[0:P, t, :]).then_inc(s_x1t, 1)

            def qk(row):
                pe.wait_ge(s_x1e, row.count())
                if row.after(1):
                    pe.wait_ge(s_qkl, row.plus(-1).count())
                for a in range(2):
                    last = pe.matmul(ps_qk[:, a * T:(a + 1) * T], w_att[:, a, :], x1t[:], start=True, stop=True)
                last.then_inc(s_qk, 1)

            def values(row):
                for t in range(NT):
                    last = pe.matmul(ps_in[0:P, t * D:(t + 1) * D], x1t[:, t * P:(t + 1) * P], w_att[:, 2, :],
                                     start=True, stop=True)
                last.then_inc(s_v, 1)

            def scores(row, h):
                if h == 0:
                    pe.wait_ge(s_stack[row.u], dma_count(row, 2))
                if h >= 2 or row.after(1):
                    pe.wait_ge(s_max, row.count(NH, h - 1))
                for t in range(NT):
                    last = pe.matmul(ps_s[h % 2][0:P, t * T:(t + 1) * T], head(0, row, h, ROWS_MAX, t * P, P),
                                     head(1, row, h, ROWS_MAX, 0, T), start=True, stop=True)
                last.then_inc(s_s, 1)

            def turn_max(row):
                pe.wait_ge(s_ml, row.count())
                if row.after(3):
                    pe.wait_ge(s_h2, row.plus(-3).count())
                pe.transpose(ps_max[0:2 * NH * NT, :], mxp[0:P, :, :].rearrange("p a h -> p (a h)"),
                             identb[0:P, 0:P]).then_inc(s_mt, 1)

            def scores_t(row, h):
                if h == 0:
                    pe.wait_ge(s_mrow[row.u], dma_count(row, 1))
                if h >= 2 or row.after(1):
                    pe.wait_ge(s_exp, row.count(NH, h - 1))
                for t in range(NT):
                    dst = ps_st[h % 2][0:P, t * T:(t + 1) * T]
                    pe.matmul(dst, head(1, row, h, ROWS_ALL, t * P, P), head(0, row, h, ROWS_ALL, 0, T),
                              start=True, stop=True)
                    last = pe.matmul(dst[:, t * P:(t + 1) * P], identb[0:P, 0:P], diag[0:P, t, :],
                                     start=False, stop=True, skip_group_check=True)
                last.then_inc(s_st, 1)

            def weigh(row, g):
                pe.wait_ge(s_exp, row.count(NH, HG * (g + 1)))
                if g == 0:
                    pe.wait_ge(s_vsb, row.count())
                    if row.after(1):
                        pe.wait_ge(s_oev, row.plus(-1).count())
                for k in range(NT):
                    for j in range(HG):
                        last = pe.matmul(ps_o[CG * j:CG * j + VW, g * T:(g + 1) * T],
                                         v_sb[0:P, row.u, k, HG * g + j, :], pt[0:P, HG * g + j, k, :],
                                         start=(k == 0), stop=(k == NT - 1))
                last.then_inc(s_pvp, 1)

            def turn_to_tokens(row):
                if row.after(1):
                    pe.wait_ge(s_sgo, row.plus(-1).count())
                pe.wait_ge(s_oev, row.count())
                for t in range(NT):
                    for g in range(2):
                        last = pe.transpose(ps_tail[0:P, (2 * t + g) * D:(2 * t + g + 1) * D],
                                            o_sb[:, g, t * P:(t + 1) * P], identf[:])
                last.then_inc(s_oq, 1)

            def turn_o(row):
                pe.wait_ge(s_on, row.count())
                turn(ps_tail, lambda t: o_n[0:P, t, :, :].rearrange("p h d -> p (h d)")).then_inc(s_ot, 1)

            def project(row):
                pe.wait_ge(s_otb, row.count())
                for t in range(NT):
                    last = pe.matmul(ps_tail[0:P, t * D:(t + 1) * D], ot[:, t * P:(t + 1) * P], w_att[:, 3, :],
                                     start=True, stop=True)
                last.then_inc(s_prj, 1)

            def turn_norm2(row):
                if row.plus(3).exists:
                    pe.wait_ge(s_mr, row.plus(3).count())
                pe.wait_ge(s_xn2, row.count(NT))
                turn(ps_tail, lambda t: xn2[0:P, t, :]).then_inc(s_x2t, 1)

            def router(row):
                pe.wait_ge(s_x2l, row.count())
                for t in range(NT):
                    dst = ps_tail[0:P, t * (1 + E):(t + 1) * (1 + E)]
                    for n, (part, w) in enumerate(((0, wrh), (0, wrl), (1, wrh))):
                        last = pe.matmul(dst, xt_all[:, row.index, part, t * P:(t + 1) * P], w[:],
                                         start=(n == 0), stop=(n == 2))
                last.then_inc(s_sg, 1)

            def iteration(i):
                emb, new, mid, nxt, old, done = (i.plus(k) for k in (4, 3, 2, 1, -1, -2))
                for h in range(NH):
                    if i.exists:
                        scores_t(i, h)
                    if mid.exists:
                        scores(mid, h)
                    if h == 0 and nxt.exists:
                        turn_max(nxt)
                    if h == 0 and new.exists:
                        turn_norm1(new)
                    if h == 1 and old.exists:
                        weigh(old, 1)
                    if h == 1 and done.exists:
                        turn_norm2(done)
                    if h == 1 and new.exists:
                        qk(new)
                    if h == 2 and new.exists:
                        values(new)
                    if h == 3 and done.exists:
                        router(done)
                    if h == 3 and old.exists:
                        turn_to_tokens(old)
                    if h == 3 and emb.exists:
                        embed(emb)
                    if h == 4 and old.exists:
                        turn_o(old)
                    if h == 5 and i.exists:
                        weigh(i, 0)
                    if h == 6 and old.exists:
                        project(old)

            run_pipeline(pe, iteration)


def experts_phase(nc, h_all, xt_all, sg_all, consts, attn_b, gate_b, w1, b1, w2, b2, out):
    with ExitStack() as ctx:
        def sb(name, shape, dt=F32):
            return ctx.enter_context(nc.sbuf_tensor(name, shape, dt))

        def sem(name):
            return ctx.enter_context(nc.semaphore(name))

        def bank(name):
            return ctx.enter_context(nc.psum_tensor(name, [D, 512], F32))

        ps_h = [bank(f"ps_h{i}") for i in range(4)]
        ps_e = [bank(f"ps_e{i}") for i in range(2)]
        ps_y = bank("ps_y")
        ps_r = bank("ps_r")

        const = sb("const2", [D, D])
        identf = const[:]
        w1s = sb("w1s", [D, E, 2, HID], BF16)
        w2s = sb("w2s", [D, E, 2, HC, D], BF16)
        w1f = sb("w1f", [D, 2, HID])
        w2f = sb("w2f", [D, 2, HC, D])
        b1f = sb("b1f", [E, HID])
        b2f = sb("b2f", [E, D])
        attn_b_col = sb("attn_b_col", [B, 1])
        gate_b_row = sb("gate_b_row", [B, E])
        ones = sb("ones", [D, D])
        iota = sb("iota", [B, E])
        tok = sb("tok", [B, T])
        tok_e = sb("tok_e", [B, T])
        tok_w = sb("tok_w", [B, T])
        small = sb("small", [B, 16])
        tok_wt = sb("tok_wt", [D, NT, B])
        pooled = sb("pooled", [D, NT, B, E])
        logit = sb("logit", [B, E])
        gate_e = sb("gate_e", [B, E])
        gate = sb("gate", [B, E])
        top = sb("top", [B, 8])
        top_i = sb("top_i", [B, 8], U32)
        top_f = sb("top_f", [B, TOPK])
        weight = sb("weight", [B, TOPK])
        spread = sb("spread", [B, TOPK, B])
        onehot = sb("onehot", [B, TOPK, E])
        onehot_t = sb("onehot_t", [E, TOPK * B])
        chosen = sb("chosen", [1, B * TOPK], U32)
        weight_bc = sb("weight_bc", [D, TOPK, B])
        b1_sel = sb("b1_sel", [D, HC, TOPK, B])
        b2_sel = sb("b2_sel", [D, TOPK, B])
        hid = sb("hid", [D, TOPK, HC, T])
        hid_h = sb("hid_h", [D, TOPK, HC, T], BF16)
        hid_l = sb("hid_l", [D, TOPK, HC, T], BF16)
        eo = sb("eo", [D, TOPK, T])
        y0 = sb("y0", [D, T])
        y = sb("y", [D, T])
        out_sb = sb("out_sb", [D, NT * D])

        s_c, s_cast = sem("router_constants"), sem("experts_split")
        s_w = [sem(f"expert_weights{i}") for i in range(2)]
        s_wh, s_cast_ones, s_oh = sem("expert_hi"), sem("router_fills"), sem("choice_spread")
        s_r, s_rv, s_ra, s_idx = sem("router_pe"), sem("router_dve"), sem("router_act"), sem("chosen_ready")
        s_h, s_hid, s_hh, s_hl = sem("hidden"), sem("hidden_gelu"), sem("hidden_hi"), sem("hidden_lo")
        s_e, s_eo, s_y, s_yt, s_o, s_w_out = (sem(n) for n in (
            "expert_out", "expert_gelu", "weighted", "weighted_turned", "out_ready", "out_written"))
        block = ctx.enter_context(nc.Block())

        @block.sync
        def _(sp):
            sp.dma_start(const[:], consts[:, 0:D]).then_inc(s_c, 16)
            sp.dma_start(attn_b_col[:], attn_b.partition_broadcast(B)).then_inc(s_c, 16)
            sp.dma_start(gate_b_row[:], gate_b.partition_broadcast(B)).then_inc(s_c, 16)
            sp.dma_start(b1f[:], b1).then_inc(s_c, 16)
            sp.dma_start(b2f[:], b2).then_inc(s_c, 16)
            for e in range(E):
                if e >= 2:
                    sp.wait_ge(s_cast, 2 * (e - 1))
                sp.dma_start(w1f[:, e % 2, :], w1[e]).then_inc(s_w[e % 2], 16)
                sp.dma_start(w2f[:, e % 2, :, :], w2[e].rearrange("(c p) o -> p c o", p=D)).then_inc(s_w[e % 2], 16)
            sp.wait_ge(s_rv, 16)
            sp.dma_start(chosen[:], top_i[:, 0:TOPK]).then_inc(s_idx, 16)
            with sp.Fori(0, B, 1) as b:
                sp.wait_ge(s_o, b + 1)
                sp.dma_start(out[b].rearrange("(t p) d -> p t d", p=P),
                             out_sb[0:P, :].rearrange("p (t d) -> p t d", t=NT)).then_inc(s_w_out, 16)
            sp.wait_ge(s_w_out, 16 * B)

        @block.gpsimd
        def _(pool):
            pool.memset(ones[:], 1.0).then_inc(s_cast_ones, 1)
            for e in range(E):
                pool.memset(iota[:, e:e + 1], float(e))
            pool.memset(small[:, 8:9], 0.0).then_inc(s_cast_ones, 1)

        @block.scalar
        def _(act):
            act.wait_ge(s_rv, 2)
            act.activation(tok_e[:], tok[:], ACT.Exp, bias=small[:, 0:1], accum_out=small[:, 1:2]).then_inc(s_ra, 1)
            act.wait_ge(s_rv, 9)
            act.activation(gate_e[:], logit[:], ACT.Exp, bias=small[:, 3:4], accum_out=small[:, 4:5]).then_inc(s_ra, 1)

            def hidden(b, k, s):
                if not isinstance(b, int) or b > 0:
                    act.wait_ge(s_hl, s - 1)
                for half in range(2):
                    act.wait_ge(s_h, s * 2 + half + 1)
                    for j in range(2):
                        c = 2 * half + j
                        last = act.activation(hid[:, k, c, :], ps_h[2 * k + half][:, j * T:(j + 1) * T], ACT.Gelu,
                                              bias=b1_sel[:, c, k, at(b)])
                    last.then_inc(s_hid, 1)

            def output(b, k, s):
                act.wait_ge(s_e, s + 1)
                if not isinstance(b, int) or b > 0:
                    act.wait_ge(s_y, s - 1)
                act.activation(eo[:, k, :], ps_e[k][:, 0:T], ACT.Gelu, bias=b2_sel[:, k, at(b)]).then_inc(s_eo, 1)

            act.wait_ge(s_rv, 19)
            run_steps(act, hidden, output)

        @block.vector
        def _(dve):
            def split(e):
                dve.wait_ge(s_w[e % 2], 32 * (e // 2 + 1))
                dve.tensor_copy(w1s[:, e, 0, :], w1f[:, e % 2, :]).then_inc(s_wh, 1)
                dve.tensor_copy(w2s[:, e, 0, :, :], w2f[:, e % 2, :, :]).then_inc(s_wh, 1)
                dve.wait_ge(s_wh, 2 * (e + 1))
                dve.tensor_tensor(w1s[:, e, 1, :], w1f[:, e % 2, :], w1s[:, e, 0, :], ALU.subtract).then_inc(s_cast, 1)
                dve.tensor_tensor(w2s[:, e, 1, :, :], w2f[:, e % 2, :, :], w2s[:, e, 0, :, :],
                                  ALU.subtract).then_inc(s_cast, 1)

            dve.wait_ge(s_c, 16 * 5)
            dve.wait_ge(s_cast_ones, 2)
            dve.wait_ge(s_r, 1)
            dve.tensor_scalar(tok[:], ps_r[0:B, 0:T], attn_b_col[:, 0:1], None, ALU.add).then_inc(s_rv, 1)
            dve.wait_ge(s_rv, 1)
            dve.tensor_reduce(small[:, 0:1], tok[:], AX_X, ALU.max, negate=True).then_inc(s_rv, 1)
            split(0)
            split(1)
            dve.wait_ge(s_ra, 1)
            dve.reciprocal(small[:, 2:3], small[:, 1:2]).then_inc(s_rv, 1)
            dve.wait_ge(s_rv, 3)
            dve.tensor_scalar(tok_w[:], tok_e[:], small[:, 2:3], None, ALU.mult).then_inc(s_rv, 1)
            dve.wait_ge(s_r, 2)
            dve.tensor_copy(tok_wt[0:P, :, :], ps_y[0:P, 0:NT * B].rearrange("p (t b) -> p t b", t=NT)).then_inc(s_rv, 1)
            dve.wait_ge(s_rv, 5)
            for t in range(NT):
                wide = tok_wt[0:P, t, :].rearrange("p (b o) -> p b o", o=1).broadcast_to([P, B, E])
                dve.tensor_tensor(pooled[0:P, t, :, :], sg_all[0:P, :, t, 1:1 + E], wide, ALU.mult).then_inc(s_rv, 1)
            dve.wait_ge(s_r, 3)
            dve.tensor_tensor(logit[:], ps_r[0:B, 256:256 + E], gate_b_row[:], ALU.add).then_inc(s_rv, 1)
            dve.wait_ge(s_rv, 8)
            dve.tensor_reduce(small[:, 3:4], logit[:], AX_X, ALU.max, negate=True).then_inc(s_rv, 1)
            dve.wait_ge(s_ra, 2)
            dve.reciprocal(small[:, 5:6], small[:, 4:5]).then_inc(s_rv, 1)
            dve.wait_ge(s_rv, 10)
            dve.tensor_scalar(gate[:], gate_e[:], small[:, 5:6], None, ALU.mult).then_inc(s_rv, 1)
            dve.wait_ge(s_rv, 11)
            dve.max(top[:], gate[:]).then_inc(s_rv, 1)
            dve.wait_ge(s_rv, 12)
            dve.max_index(top_i[:], top[:], gate[:]).then_inc(s_rv, 1)
            dve.tensor_reduce(small[:, 6:7], top[:, 0:TOPK], AX_X, ALU.add).then_inc(s_rv, 1)
            dve.wait_ge(s_rv, 14)
            dve.tensor_scalar(small[:, 7:8], small[:, 6:7], 1e-9, None, ALU.add).then_inc(s_rv, 1)
            dve.tensor_copy(top_f[:], top_i[:, 0:TOPK]).then_inc(s_rv, 1)
            dve.wait_ge(s_rv, 16)
            dve.reciprocal(small[:, 9:10], small[:, 7:8]).then_inc(s_rv, 1)
            for k in range(TOPK):
                last = dve.tensor_scalar(onehot[:, k, :], iota[:], top_f[:, k:k + 1], None, ALU.is_equal)
            last.then_inc(s_oh, 1)
            dve.wait_ge(s_rv, 17)
            dve.tensor_scalar(weight[:], top[:, 0:TOPK], small[:, 9:10], None, ALU.mult).then_inc(s_oh, 1)
            dve.wait_ge(s_oh, 2)
            for k in range(TOPK):
                last = dve.tensor_scalar(spread[:, k, :], identf[0:B, 0:B], weight[:, k:k + 1], None, ALU.mult)
            last.then_inc(s_oh, 1)
            dve.wait_ge(s_r, 4)
            dve.tensor_copy(onehot_t[:], ps_y[0:E, 0:TOPK * B]).then_inc(s_oh, 1)
            dve.wait_ge(s_r, 5)
            dve.tensor_copy(weight_bc[:].rearrange("p k b -> p (k b)"), ps_r[:, 0:TOPK * B]).then_inc(s_oh, 1)
            dve.wait_ge(s_r, 6)
            dve.tensor_copy(b1_sel[:].rearrange("p c k b -> p (c k b)"), ps_y[:, 0:HC * TOPK * B]).then_inc(s_rv, 1)
            dve.tensor_copy(b2_sel[:].rearrange("p k b -> p (k b)"), ps_r[:, 128:128 + TOPK * B]).then_inc(s_rv, 1)
            for e in range(2, E):
                split(e)

            def hidden(b, k, s):
                dve.wait_ge(s_hid, s * 2 + 2)
                if not isinstance(b, int) or b > 0:
                    dve.wait_ge(s_e, s - 1)
                dve.tensor_copy(hid_h[:, k, :, :], hid[:, k, :, :]).then_inc(s_hh, 1)
                dve.wait_ge(s_hh, s + 1)
                dve.tensor_tensor(hid_l[:, k, :, :], hid[:, k, :, :], hid_h[:, k, :, :], ALU.subtract).then_inc(s_hl, 1)

            def output(b, k, s):
                dve.wait_ge(s_eo, s + 1)
                if k == 0:
                    if not isinstance(b, int) or b > 0:
                        dve.wait_ge(s_y, s)
                    dve.tensor_scalar(y0[:], eo[:, 0, :], weight_bc[:, 0, at(b)], None, ALU.mult).then_inc(s_y, 1)
                    return
                dve.wait_ge(s_y, s)
                if not isinstance(b, int) or b > 0:
                    dve.wait_ge(s_yt, b)
                dve.scalar_tensor_tensor(y[:], eo[:, 1, :], weight_bc[:, 1, at(b)], y0[:], ALU.mult,
                                         ALU.add).then_inc(s_y, 1)

            def finish(b):
                dve.wait_ge(s_yt, b + 1)
                if not isinstance(b, int) or b > 0:
                    dve.wait_ge(s_w_out, 16 * b)
                dve.tensor_tensor(out_sb[0:P, :], ps_y[0:P, 0:NT * D], h_all[0:P, b, :], ALU.add).then_inc(s_o, 1)

            run_steps(dve, hidden, output, finish)

        @block.tensor
        def _(pe):
            pe.wait_ge(s_c, 16 * 5)
            pe.wait_ge(s_cast_ones, 2)
            for t in range(NT):
                last = pe.transpose(ps_r[0:B, t * P:(t + 1) * P], sg_all[0:P, :, t, 0], identf[0:P, 0:P])
            last.then_inc(s_r, 1)
            pe.wait_ge(s_rv, 4)
            for t in range(NT):
                last = pe.transpose(ps_y[0:P, t * B:(t + 1) * B], tok_w[:, t * P:(t + 1) * P], identf[0:B, 0:B])
            last.then_inc(s_r, 1)
            pe.wait_ge(s_rv, 7)
            for e in range(E):
                for t in range(NT):
                    last = pe.matmul(ps_r[0:B, 256 + e:257 + e], pooled[0:P, t, :, e], ones[0:P, 0:1],
                                     start=(t == 0), stop=(t == NT - 1))
            last.then_inc(s_r, 1)
            pe.wait_ge(s_oh, 1)
            for k in range(TOPK):
                last = pe.transpose(ps_y[0:E, k * B:(k + 1) * B], onehot[:, k, :], identf[0:B, 0:B])
            last.then_inc(s_r, 1)
            pe.wait_ge(s_oh, 3)
            for k in range(TOPK):
                last = pe.matmul(ps_r[:, k * B:(k + 1) * B], ones[0:B, :], spread[:, k, :], start=True, stop=True)
            last.then_inc(s_r, 1)
            pe.wait_ge(s_oh, 5)
            for c in range(HC):
                pe.matmul(ps_y[:, c * TOPK * B:(c + 1) * TOPK * B], b1f[:, c * D:(c + 1) * D], onehot_t[:],
                          start=True, stop=True)
            pe.matmul(ps_r[:, 128:128 + TOPK * B], b2f[:], onehot_t[:], start=True, stop=True).then_inc(s_r, 1)
            pe.wait_ge(s_rv, 19)
            pe.wait_ge(s_cast, 2 * E)
            pe.wait_ge(s_idx, 16)

            def hidden(b, k, s):
                e = pe.value_load(chosen[0:1, at(s)], min_val=0, max_val=E - 1)
                if not isinstance(b, int) or b > 0:
                    pe.wait_ge(s_hid, s * 2 - 2)
                for half in range(2):
                    for j in range(2):
                        c = 2 * half + j
                        dst = ps_h[2 * k + half][:, j * T:(j + 1) * T]
                        for n, (wp, xp) in enumerate(((0, 0), (0, 1), (1, 0))):
                            last = pe.matmul(dst, w1s[:, e, wp, c * D:(c + 1) * D], xt_all[:, b, xp, :],
                                             start=(n == 0), stop=(n == 2))
                    last.then_inc(s_h, 1)

            def output(b, k, s):
                e = pe.value_load(chosen[0:1, at(s)], min_val=0, max_val=E - 1)
                pe.wait_ge(s_hl, s + 1)
                if not isinstance(b, int) or b > 0:
                    pe.wait_ge(s_eo, s - 1)
                for c in range(HC):
                    for n, (wp, part) in enumerate(((0, hid_h), (0, hid_l), (1, hid_h))):
                        last = pe.matmul(ps_e[k][:, 0:T], w2s[:, e, wp, c, :], part[:, k, c, :],
                                         start=(c == 0 and n == 0), stop=(c == HC - 1 and n == 2))
                last.then_inc(s_e, 1)

            def finish(b):
                pe.wait_ge(s_y, b * 2 + 2)
                if not isinstance(b, int) or b > 0:
                    pe.wait_ge(s_o, b)
                for t in range(NT):
                    last = pe.transpose(ps_y[0:P, t * D:(t + 1) * D], y[:, t * P:(t + 1) * P], identf)
                last.then_inc(s_yt, 1)

            run_steps(pe, hidden, output, finish)


def at(i):
    return slice(i, i + 1) if isinstance(i, int) else bass.ds(i, 1)


def run_steps(eng, hidden, output, finish=None):
    def row(b, first=False, last=False):
        for k in range(TOPK):
            if not last:
                hidden(b + 1, k, b * 2 + 2 + k)
            output(b, k, b * 2 + k)
            if k == 0 and finish is not None and not first:
                finish(b - 1)

    hidden(0, 0, 0)
    hidden(0, 1, 1)
    row(0, first=True)
    with eng.Fori(1, B - 1, 1) as b:
        row(b)
    row(B - 1, last=True)
    if finish is not None:
        finish(B - 1)


def bass_audio_tower(nc, consts, x, W_ve, W_lin_T, b_ve, b_lin, w_qkv_T, w_out_T, b_out,
                     attn_w, attn_b, gate_w, gate_b, w1, b1, w2, b2, out):
    with ExitStack() as ctx:
        h_all = ctx.enter_context(nc.sbuf_tensor("h_all", [D, B, NT * D], F32))
        xt_all = ctx.enter_context(nc.sbuf_tensor("xt_all", [D, B, 2, T], BF16))
        sg_all = ctx.enter_context(nc.sbuf_tensor("sg_all", [D, B, NT, 1 + E], F32))
        attention_phase(nc, h_all, xt_all, sg_all, consts, x, W_ve, W_lin_T, b_ve, b_lin, w_qkv_T,
                        w_out_T, b_out, attn_w, gate_w)
        experts_phase(nc, h_all, xt_all, sg_all, consts, attn_b, gate_b, w1, b1, w2, b2, out)


_INS = ["x", "W_ve", "W_lin_T", "b_ve", "b_lin", "w_qkv_T", "w_out_T", "b_out", "attn_w", "attn_b",
        "gate_w", "gate_b", "w1", "b1", "w2", "b2"]


def kernel(x, L0_tok_W_ve, L0_tok_b_ve, L0_tok_W_lin, L0_tok_b_lin, L0_attn_w_qkv, L0_attn_w_out,
           L0_attn_b_out, L0_ffn_attn_w, L0_ffn_attn_b, L0_ffn_gate_w, L0_ffn_gate_b, L0_ffn_w1,
           L0_ffn_b1, L0_ffn_w2, L0_ffn_b2):
    import concourse.bacc as bacc
    from concourse.bass_utils import run_bass_kernel_spmd

    qkv = np.asarray(L0_attn_w_qkv)
    qk = qkv[:2 * D].reshape(2, NH, HD, D).transpose(0, 2, 1, 3).reshape(2 * D, D)
    qkv_T = np.concatenate([qk, qkv[2 * D:]]).T

    laid_out = {
        "consts": constants(), "x": x, "W_ve": L0_tok_W_ve, "W_lin_T": np.asarray(L0_tok_W_lin).T,
        "b_ve": L0_tok_b_ve, "b_lin": L0_tok_b_lin, "w_qkv_T": qkv_T,
        "w_out_T": np.asarray(L0_attn_w_out).T, "b_out": L0_attn_b_out, "attn_w": L0_ffn_attn_w,
        "attn_b": L0_ffn_attn_b, "gate_w": L0_ffn_gate_w, "gate_b": L0_ffn_gate_b, "w1": L0_ffn_w1,
        "b1": L0_ffn_b1, "w2": L0_ffn_w2, "b2": L0_ffn_b2,
    }
    nc = bacc.Bacc("TRN2", target_bir_lowering=False, num_devices=1)
    arrays, args = {}, []
    for name, a in laid_out.items():
        a = np.ascontiguousarray(a)
        arrays[f"in_{name}"] = a
        args.append(nc.dram_tensor(f"in_{name}", a.shape, mybir.dt.from_np(a.dtype), kind="ExternalInput").ap())
    args.append(nc.dram_tensor("out_h", (B, T, D), F32, kind="ExternalOutput").ap())
    bass_audio_tower(nc, *args)
    got = run_bass_kernel_spmd(nc, [arrays], core_ids=[0])
    return got.results[0]["out_h"]
```

```python
import math
from contextlib import ExitStack

import numpy as np

import concourse.bass as bass
from concourse import mybir

F32 = mybir.dt.float32
BF16 = mybir.dt.bfloat16
U32 = mybir.dt.uint32
ALU = mybir.AluOpType
ACT = mybir.ActivationFunctionType
AX_X = mybir.AxisListType.X

B, C, T = 64, 32, 250
D = 128
NH, HD = 8, 16
E, HID, TOPK = 8, 512, 2
P = 125
NT = T // P
U = 4
HC = HID // D
VW = HD + 1
RING = 4
ROWS_C = 4
STAGE = 3

ALPHA = 0.1
LAMBDA = -math.log(0.9)
Q_SCALE = 1.0 / (math.sqrt(HD) * LAMBDA)
EPS = 1e-5

ROWS_DOT, ROWS_MAX = 3 * HD, 96
ROW_K, ROW_1, ROW_M = ROWS_MAX, ROWS_MAX + 1, ROWS_MAX + 2
ROWS_ALL = ROWS_MAX + 4
HG = 4
CG = D // HG

def constants():
    k = np.arange(P)[:, None]
    q = np.arange(P)[None, :]
    ident = np.eye(D, dtype=np.float32)
    diag = np.zeros((D, NT, P), np.float32)
    diag[:P, 0] = np.maximum(k - q, 0)
    diag[:P, 1] = np.maximum(q - k, 0)
    qrows = np.zeros((D, T), np.float32)
    krows = np.zeros((D, T), np.float32)
    krows[ROW_K, :P] = -np.arange(P)
    qrows[ROW_K] = 1
    krows[ROW_1, :P] = 1
    qrows[ROW_1] = np.arange(T)
    krows[ROW_M:ROW_M + 2] = -1
    return np.ascontiguousarray(np.concatenate([ident, diag.reshape(D, -1), qrows, krows], axis=1))


class Row:

    def __init__(self, first, u):
        self.first, self.u = first, u

    def plus(self, k):
        carry, u = divmod(self.u + k, U)
        return Row(self.first + U * carry if carry else self.first, u)

    @property
    def static(self):
        return isinstance(self.first, int)

    def count(self, each=1, upto=None):
        upto = each if upto is None else upto
        return self.first * each + (self.u * each + upto)

    @property
    def index(self):
        return self.first + self.u if self.u or self.static else self.first

    @property
    def exists(self):
        return not self.static or 0 <= self.first + self.u < B

    def after(self, k):
        return not self.static or self.first + self.u - k >= 0


def run_pipeline(eng, iteration):
    for i in range(-4, U):
        iteration(Row(0, 0).plus(i))
    with eng.Fori(U, B - 2 * U, U) as first:
        for u in range(U):
            iteration(Row(first, u))
    for i in range(B - 2 * U, B + 2):
        iteration(Row(0, 0).plus(i))


def dma_count(row, each):
    return 16 * each * (row.first // U + 1) if row.static else row.first * (16 * each // U) + 16 * each


def precedes_group(row, u):
    return row.exists and row.u == u and (not row.static or row.first + U < B)


def attention_phase(nc, h_all, xt_all, sg_all, identf, attn_b_col, gate_b_row, consts, x, W_ve, W_lin_T,
                    b_ve, b_lin, w_qkv_T, w_out_T, b_out, attn_w, attn_b, gate_w, gate_b):
    with ExitStack() as ctx:
        def sb(name, shape, dt=F32):
            return ctx.enter_context(nc.sbuf_tensor(name, shape, dt))

        def sem(name):
            return ctx.enter_context(nc.semaphore(name))

        def bank(name):
            return ctx.enter_context(nc.psum_tensor(name, [D, 512], F32))

        ps_s = [bank(f"ps_s{i}") for i in range(2)]
        ps_st = [bank(f"ps_st{i}") for i in range(2)]
        ps_in = bank("ps_in")
        ps_max = ps_in[:, 0:P].bitcast(BF16)[:, 0:P]
        ps_qk = bank("ps_qk")
        ps_o = bank("ps_o")
        ps_tail = bank("ps_tail")

        identb = sb("identb", [D, D], BF16)
        diag = sb("diag", [D, NT, P], BF16)
        stacks = sb("stacks", [D, RING, 2, NH, T], BF16)
        x_raw = sb("x_raw", [D, T])
        x_diff = sb("x_diff", [D, T])
        x_left = sb("x_left", [D, T])
        x_sum = sb("x_sum", [D, T])
        keep = sb("keep", [D, 1])
        starts = sb("starts", [D, 2])
        w_emb = sb("w_emb", [D, U, D])
        bias_in = sb("bias_in", [D, D])
        b_out_row = sb("b_out_row", [D, D])
        w_att = sb("w_att", [D, 4, D])
        wrf = sb("wrf", [D, 1 + E])
        wrh = sb("wrh", [D, 1 + E], BF16)
        wrl = sb("wrl", [D, 1 + E], BF16)
        power = sb("power", [D, NT])
        h_raw = sb("h_raw", [D, NT, D])
        h_in = sb("h_in", [D, NT, D])
        st1, st2 = sb("st1", [D, NT, 6]), sb("st2", [D, NT, 6])
        mv1, mv2 = sb("mv1", [D, NT, 2]), sb("mv2", [D, NT, 2])
        ve1, ve2 = sb("ve1", [D, 2, NT]), sb("ve2", [D, 2, NT])
        rs1, rs2 = sb("rs1", [D, 2, NT]), sb("rs2", [D, 2, NT])
        xn1, xn2 = sb("xn1", [D, NT, D]), sb("xn2", [D, NT, D])
        x1t = sb("x1t", [D, T])
        parts = sb("parts", [D, 4, T], BF16)
        v_sb = sb("v_sb", [D, RING, NT, NH, VW])
        mx = sb("mx", [D, NH * NT])
        mxp = sb("mxp", [D, 2, NH * NT], BF16)
        mxt = sb("mxt", [2 * NH * NT, P], BF16)
        pt = sb("pt", [D, NH, NT, T])
        o_sb = sb("o_sb", [D, 2, T])
        o_rec = sb("o_rec", [D, NT, NH])
        o_n = sb("o_n", [D, NT, NH, HD])
        ot = sb("ot", [D, T])

        spare = xt_all[:, B - 8:B, :, :].rearrange("p b a t -> p (b a t)").bitcast(F32)
        const = spare[:, 0:D + NT * P + 2 * T]
        q_rows, k_rows = (const[:, D + NT * P + i * T:D + NT * P + (i + 1) * T] for i in range(2))
        at0 = D + NT * P + 2 * T
        w_linT = spare[:, at0:at0 + D]
        b_ve_wide = spare[:, at0 + D:at0 + 2 * D]
        b_lin_row = spare[:, at0 + 2 * D:at0 + 3 * D]
        w_q_raw = spare[:, at0 + 3 * D:at0 + 4 * D]
        w_ve_wide = spare[:, at0 + 4 * D:at0 + 5 * D]
        b_ve_col = spare[:, at0 + 5 * D:at0 + 5 * D + 1]

        scratch = [nc.dram_tensor(f"scratch{i}", (4, D, T), BF16, kind="Internal").ap() for i in range(2)]

        s_parts = [sem(f"parts_in_dram{i}") for i in range(RING)]
        s_const, s_w, s_x = sem("consts_loaded"), sem("weights_loaded"), sem("x_loaded")
        s_router = sem("router_biases_loaded")
        s_stack = [sem(f"stack_in_place{i}") for i in range(RING)]
        s_mrow = [sem(f"max_rows_in_place{i}") for i in range(RING)]
        s_prep, s_pv, s_pw = sem("prepared_vector"), sem("prepared_pool"), sem("embedding_product")
        s_keep, s_wv = sem("vector_constants"), sem("weights_ready")
        s_diff, s_scan, s_smooth = sem("x_diff_made"), sem("x_scans"), sem("x_smoothed")
        s_ends = sem("x_ends")
        (s_emb, s_hraw, s_hin, s_hres, s_st1, s_ag1, s_ve1, s_rp1, s_rs1, s_xn1, s_x1t, s_x1e, s_qk,
         s_qkh, s_qkl, s_v, s_vsb) = (sem(n) for n in (
            "embedded", "embedding_out", "bias_added", "residual_kept", "stats1", "aggr1", "var1",
            "power1", "rstd1", "norm1", "norm1_turned", "norm1_out", "qk_product", "qk_hi", "qk_lo",
            "v_product", "v_out"))
        (s_s, s_max, s_mh, s_ml, s_mt, s_mr, s_st, s_exp, s_pvp) = (sem(n) for n in (
            "scores", "score_max", "max_hi", "max_lo", "max_turned", "max_rows", "scores_t",
            "exp_done", "pv_product"))
        (s_oev, s_oq, s_rec, s_on, s_ot, s_otb, s_prj, s_h2, s_st2, s_ag2, s_ve2, s_rp2, s_rs2, s_xn2,
         s_x2t, s_x2h, s_x2l, s_sg, s_sgo) = (sem(n) for n in (
            "o_out", "o_by_token", "recip", "o_normed", "o_turned", "o_turned_out", "o_projected",
            "h2_made", "stats2", "aggr2", "var2", "power2", "rstd2", "norm2", "norm2_turned",
            "norm2_hi", "norm2_lo", "router_product", "router_out"))

        def head(which, row, h, rows, lo, n):
            return stacks[0:rows, row.u, which, h, lo:lo + n]

        def x_group(group):
            return x.rearrange("(g q) c t -> g (q c) t", q=U)[group]

        def wide(a, n=NT):
            return a.rearrange("p (o d) -> p o d", o=1).broadcast_to([a.shape[0], n, a.shape[1]])

        block = ctx.enter_context(nc.Block())

        @block.sync
        def _(sp):
            sp.dma_start(const, consts).then_inc(s_const, 16)
            sp.dma_start(identf[:], consts[:, 0:D]).then_inc(s_const, 16)
            sp.dma_start(x_raw[:], x_group(0)).then_inc(s_x, 16)
            sp.dma_start(w_ve_wide.rearrange("p (q c) -> p q c", q=U),
                         W_ve.rearrange("d (o c) -> d o c", o=1).broadcast_to([D, U, C])).then_inc(s_w, 16)
            sp.dma_start(w_linT, W_lin_T).then_inc(s_w, 16)
            sp.dma_start(b_ve_col, b_ve.rearrange("(d o) -> d o", o=1)).then_inc(s_w, 16)
            sp.dma_start(b_lin_row, b_lin.partition_broadcast(D)).then_inc(s_w, 16)
            sp.dma_start(b_out_row[:], b_out.partition_broadcast(D)).then_inc(s_w, 16)
            sp.dma_start(w_q_raw, w_qkv_T[:, 0:D]).then_inc(s_w, 16)
            sp.dma_start(w_att[:, 1:3, :], w_qkv_T[:, D:3 * D].rearrange("p (a d) -> p a d", a=2)).then_inc(s_w, 16)
            sp.dma_start(w_att[:, 3, :], w_out_T).then_inc(s_w, 16)
            sp.dma_start(wrf[:, 0:1], attn_w).then_inc(s_w, 16)
            sp.dma_start(wrf[:, 1:1 + E], gate_w).then_inc(s_w, 16)
            sp.dma_start(attn_b_col[:], attn_b.partition_broadcast(B)).then_inc(s_router, 16)
            sp.dma_start(gate_b_row[:], gate_b.partition_broadcast(B)).then_inc(s_router, 16)
            sp.wait_ge(s_router, 16 * 2)
            sp.wait_ge(s_keep, 2 + 2 * RING)

            def max_rows(row):
                sp.wait_ge(s_mr, row.count())
                sp.dma_start(stacks[ROW_M:ROW_M + 2, row.u, 0, :, :].rearrange("r h (t p) -> r (h t) p", t=NT),
                             mxt[:]).then_inc(s_mrow[row.u], 16)

            def parts_out(row):
                sp.wait_ge(s_qkh, row.count())
                sp.wait_ge(s_qkl, row.count())
                sp.dma_start(scratch[row.u % 2].rearrange("g p t -> p g t"), parts[:]).then_inc(s_parts[row.u], 16)

            def stack(row):
                sp.wait_ge(s_parts[row.u], dma_count(row, 1))
                for which, to, first, n in ((0, 0, 0, 2), (1, 0, 2, 1), (0, 2, 1, 1), (1, 1, 2, 2)):
                    sp.dma_start(stacks[to * HD:(to + n) * HD, row.u, which, :, :],
                                 scratch[row.u % 2][first:first + n].rearrange("g (d h) t -> g d (h t)", d=HD)
                                 ).then_inc(s_stack[row.u], 16)

            def iteration(i):
                emb, new, nxt = i.plus(4), i.plus(3), i.plus(1)
                if new.exists:
                    parts_out(new)
                if nxt.exists:
                    max_rows(nxt)
                if new.exists:
                    stack(new)
                if precedes_group(emb, 0):
                    sp.wait_ge(s_diff, emb.first // U + 1)
                    sp.dma_start(x_raw[:], x_group(emb.first // U + 1)).then_inc(s_x, 16)

            run_pipeline(sp, iteration)

        @block.gpsimd
        def _(pool):
            pool.memset(power[:], -0.5).then_inc(s_pv, 1)
            pool.memset(v_sb[:], 1.0).then_inc(s_pv, 1)
            pool.wait_ge(s_pv, 2)
            pool.wait_ge(s_w, 16 * 10)
            pool.wait_ge(s_pw, 2)

            def embed_out(row):
                pool.wait_ge(s_hraw, row.count())
                if row.after(1):
                    pool.wait_ge(s_xn1, row.plus(-1).count(NT))
                    pool.wait_ge(s_hres, row.plus(-1).count())
                pool.tensor_tensor(h_in[0:P, :, :], h_raw[0:P, :, :], wide(bias_in[0:P, :]), ALU.add).then_inc(s_hin, 1)

            def keep_residual(row):
                pool.wait_ge(s_hin, row.count())
                pool.tensor_tensor(h_all[0:P, row.index, :].rearrange("p (t d) -> p t d", t=NT), h_in[0:P, :, :],
                                   wide(b_out_row[0:P, :]), ALU.add).then_inc(s_hres, 1)

            def deviation(row, ve, rs, s_var, s_pow, s_rs):
                pool.wait_ge(s_var, row.count(2))
                pool.tensor_tensor(rs[0:P, 0, :], ve[0:P, 0, :], power[0:P, :], ALU.pow).then_inc(s_pow, 1)
                pool.wait_ge(s_pow, row.count())
                pool.tensor_tensor(rs[0:P, 1, :], ve[0:P, 1, :], rs[0:P, 0, :], ALU.mult).then_inc(s_rs, 1)

            def iteration(i):
                emb, done = i.plus(4), i.plus(-2)
                if emb.exists:
                    embed_out(emb)
                if done.exists:
                    deviation(done, ve2, rs2, s_ve2, s_rp2, s_rs2)
                if emb.exists:
                    deviation(emb, ve1, rs1, s_ve1, s_rp1, s_rs1)
                    keep_residual(emb)

            run_pipeline(pool, iteration)

        @block.scalar
        def _(act):
            act.wait_ge(s_const, 32)
            for r in range(RING):
                act.copy(stacks[:, r, 1, :, :], wide(k_rows, NH)).then_inc(s_keep, 1)
            act.wait_ge(s_pv, 2)

            def embed_out(row):
                act.wait_ge(s_emb, row.count())
                if row.after(1):
                    act.wait_ge(s_hin, row.plus(-1).count())
                act.copy(h_raw[0:P, :, :].rearrange("p t d -> p (t d)"), ps_in[0:P, 0:NT * D]).then_inc(s_hraw, 1)

            def normed(row, src, rs, xn, s_rs, s_turned, s_done):
                act.wait_ge(s_rs, row.count())
                if row.after(1):
                    act.wait_ge(s_turned, row.plus(-1).count())
                for t in range(NT):
                    act.activation(xn[0:P, t, :], src(t), ACT.Identity, bias=rs[0:P, 1, t:t + 1],
                                   scale=rs[0:P, 0, t:t + 1]).then_inc(s_done, 1)

            def norm1_out(row):
                act.wait_ge(s_x1t, row.count())
                if row.after(1):
                    act.wait_ge(s_v, row.plus(-1).count())
                act.copy(x1t[:], ps_in[:, 0:T]).then_inc(s_x1e, 1)

            def qk_hi(row):
                act.wait_ge(s_qk, row.count())
                if row.after(1):
                    act.wait_ge(s_parts[(row.u - 1) % RING], dma_count(row.plus(-1), 1))
                act.copy(parts[:, 1:3, :], ps_qk[:, 0:2 * T].rearrange("p (a t) -> p a t", a=2)).then_inc(s_qkh, 1)

            def v_out(row):
                act.wait_ge(s_v, row.count())
                act.copy(v_sb[0:P, row.u, :, :, 0:HD],
                         ps_tail[0:P, 0:NT * D].rearrange("p (t h d) -> p t h d", t=NT, h=NH)).then_inc(s_vsb, 1)

            def exps(row, h):
                act.wait_ge(s_st, row.count(NH, h + 1))
                if h % HG == 0 and row.after(1):
                    act.wait_ge(s_pvp, row.plus(-1).count(2, h // HG + 1))
                act.activation(pt[0:P, h, :, :].rearrange("p a t -> p (a t)"),
                               ps_st[h % 2][0:P, 0:NT * T], ACT.Exp, scale=LAMBDA).then_inc(s_exp, 1)

            def max_out(row):
                act.wait_ge(s_mt, row.count())
                if row.after(1):
                    act.wait_ge(s_mrow[(row.u - 1) % RING], dma_count(row.plus(-1), 1))
                act.copy(mxt[:], ps_max[0:2 * NH * NT, :]).then_inc(s_mr, 1)

            def o_out(row, g):
                act.wait_ge(s_pvp, row.count(2, g + 1))
                if row.after(1):
                    act.wait_ge(s_oq, row.plus(-1).count())
                act.copy(o_sb[:, g, :], ps_o[:, 0:T]).then_inc(s_oev, 1)

            def o_turned_out(row):
                act.wait_ge(s_ot, row.count())
                if row.after(1):
                    act.wait_ge(s_prj, row.plus(-1).count())
                act.copy(ot[:], ps_tail[:, 0:T]).then_inc(s_otb, 1)

            def norm2_hi(row):
                act.wait_ge(s_x2t, row.count())
                act.copy(xt_all[:, row.index, 0, :], ps_qk[:, 0:T]).then_inc(s_x2h, 1)

            def iteration(i):
                emb, new, nxt, old, done = i.plus(4), i.plus(3), i.plus(1), i.plus(-1), i.plus(-2)
                for h in range(NH):
                    if i.exists:
                        exps(i, h)
                    if h == 0 and new.exists:
                        qk_hi(new)
                    if h == 1 and emb.exists:
                        embed_out(emb)
                    if h == 2 and old.exists:
                        o_out(old, 1)
                    if h == 2 and new.exists:
                        v_out(new)
                    if h == 3 and nxt.exists:
                        max_out(nxt)
                    if h == 3 and done.exists:
                        normed(done, lambda t: h_all[0:P, done.index, t * D:(t + 1) * D], rs2, xn2, s_rs2, s_x2t, s_xn2)
                    if h == 4 and emb.exists:
                        normed(emb, lambda t: h_in[0:P, t, :], rs1, xn1, s_rs1, s_x1t, s_xn1)
                    if h == 4 and done.exists:
                        norm2_hi(done)
                    if h == 5 and old.exists:
                        o_turned_out(old)
                    if h == 5 and i.exists:
                        o_out(i, 0)
                    if h == 6 and emb.exists:
                        norm1_out(emb)

            run_pipeline(act, iteration)

        @block.vector
        def _(dve):
            dve.memset(keep[:], 1.0 - ALPHA).then_inc(s_prep, 1)
            dve.memset(x_diff[:, 0:1], 0.0).then_inc(s_prep, 1)
            dve.memset(w_emb[:], 0.0).then_inc(s_prep, 1)
            dve.memset(ps_o[:, 0:T], 0.0).then_inc(s_prep, 1)
            dve.wait_ge(s_const, 32)
            dve.tensor_copy(identb[:], identf[:]).then_inc(s_keep, 1)
            dve.tensor_copy(diag[:].rearrange("p a t -> p (a t)"), const[:, D:D + NT * P]).then_inc(s_keep, 1)
            for r in range(RING):
                dve.tensor_copy(stacks[:, r, 0, :, :], wide(q_rows, NH)).then_inc(s_keep, 1)
            dve.wait_ge(s_w, 16 * 10)
            dve.tensor_scalar(w_att[:, 0, :], w_q_raw, Q_SCALE, None, ALU.mult).then_inc(s_wv, 1)
            dve.tensor_copy(wrh[:], wrf[:]).then_inc(s_wv, 1)
            dve.wait_ge(s_wv, 2)
            dve.tensor_tensor(wrl[:], wrf[:], wrh[:], ALU.subtract).then_inc(s_wv, 1)
            dve.tensor_scalar(b_ve_wide, identf[:], 0.0, b_ve_col, ALU.mult, ALU.add).then_inc(s_wv, 1)
            dve.wait_ge(s_pw, 1)
            dve.wait_ge(s_prep, 4)
            dve.tensor_tensor(bias_in[:], ps_in[:, D:2 * D], b_lin_row, ALU.add).then_inc(s_pw, 1)
            for q in range(U):
                r = slice(q * C, (q + 1) * C)
                dve.tensor_scalar(w_emb[r, q, :], ps_in[r, 0:D], ALPHA / 2, None, ALU.mult).then_inc(s_pw, 1)

            kept = keep[:].broadcast_to([D, T - 1])

            def differences(group):
                dve.wait_ge(s_x, group * 16 + 16)
                dve.tensor_tensor(x_diff[:, 1:T], x_raw[:, 1:T], x_raw[:, 0:T - 1], ALU.subtract).then_inc(s_diff, 1)
                dve.wait_ge(s_diff, group + 1)
                dve.tensor_scalar(starts[:], x_diff[:, 0:T:T - 1], 1.0 / ALPHA, None, ALU.mult).then_inc(s_ends, 1)

            def average_forward(group):
                dve.wait_ge(s_ends, group * 3 + 1)
                dve.tensor_tensor_scan(x_left[:, 1:T], kept, x_diff[:, 1:T], starts[:, 0:1],
                                       ALU.mult, ALU.add).then_inc(s_scan, 1)
                dve.tensor_copy(x_left[:, 0:1], starts[:, 0:1]).then_inc(s_ends, 1)

            def average_backward(group):
                dve.wait_ge(s_scan, group * 2 + 1)
                dve.tensor_tensor_scan(x_diff[:, T - 2::-1], kept, x_diff[:, T - 2::-1], starts[:, 1:2],
                                       ALU.mult, ALU.add).then_inc(s_scan, 1)
                dve.tensor_copy(x_diff[:, T - 1:T], starts[:, 1:2]).then_inc(s_ends, 1)

            def both_averages(group, last_row):
                dve.wait_ge(s_scan, group * 2 + 2)
                dve.wait_ge(s_ends, group * 3 + 3)
                if last_row is not None:
                    dve.wait_ge(s_emb, last_row.count())
                dve.tensor_tensor(x_sum[:], x_left[:], x_diff[:], ALU.add).then_inc(s_smooth, 1)
                dve.wait_ge(s_smooth, group * 2 + 1)
                dve.memset(x_diff[:, 0:1], 0.0).then_inc(s_smooth, 1)

            def score_max(row, h):
                dve.wait_ge(s_s, row.count(NH, h + 1))
                if h == 0 and row.after(1):
                    dve.wait_ge(s_ml, row.plus(-1).count())
                dve.tensor_reduce(mx[0:P, h * NT:(h + 1) * NT],
                                  ps_s[h % 2][0:P, 0:NT * T].rearrange("p (a t) -> p a t", a=NT),
                                  AX_X, ALU.max).then_inc(s_max, 1)

            def max_parts(row):
                dve.wait_ge(s_max, row.count(NH))
                if row.after(1):
                    dve.wait_ge(s_mt, row.plus(-1).count())
                dve.tensor_copy(mxp[0:P, 0, :], mx[0:P, :]).then_inc(s_mh, 1)
                dve.wait_ge(s_mh, row.count())
                dve.tensor_tensor(mxp[0:P, 1, :], mx[0:P, :], mxp[0:P, 0, :], ALU.subtract).then_inc(s_ml, 1)

            def stats(row, src, st, s_stat):
                for t in range(NT):
                    dve.bn_stats(st[0:P, t, :], src(t)).then_inc(s_stat, 1)

            def aggregate(row, st, mv, ve, s_agg, s_var):
                for t in range(NT):
                    dve.bn_aggr(mv[0:P, t, :], st[0:P, t, :]).then_inc(s_agg, 1)
                dve.wait_ge(s_agg, row.count(NT))
                dve.tensor_scalar(ve[0:P, 0, :], mv[0:P, :, 1], EPS, None, ALU.add).then_inc(s_var, 1)
                dve.tensor_scalar(ve[0:P, 1, :], mv[0:P, :, 0], -1.0, None, ALU.mult).then_inc(s_var, 1)

            def low(row, dst, psum, hi, s_hi, s_lo):
                dve.wait_ge(s_hi, row.count())
                dve.tensor_tensor(dst, psum, hi, ALU.subtract).then_inc(s_lo, 1)

            def o_normed(row):
                dve.wait_ge(s_oq, row.count())
                o = ps_tail[0:P, :].rearrange("p (t h d) -> p t h d", t=NT, h=NH)
                dve.reciprocal(o_rec[0:P, :, :], o[:, :, :, HD]).then_inc(s_rec, 1)
                dve.wait_ge(s_rec, row.count())
                rec = o_rec[0:P, :, :].rearrange("p t (h o) -> p t h o", o=1).broadcast_to([P, NT, NH, HD])
                dve.tensor_tensor(o_n[0:P, :, :, :], o[:, :, :, 0:HD], rec, ALU.mult).then_inc(s_on, 1)

            def residual(row):
                dve.wait_ge(s_prj, row.count())
                dve.wait_ge(s_hres, row.count())
                h = h_all[0:P, row.index, :]
                dve.tensor_tensor(h, ps_tail[0:P, 0:NT * D], h, ALU.add).then_inc(s_h2, 1)

            def router_out(row):
                dve.wait_ge(s_sg, row.count())
                dve.tensor_copy(sg_all[0:P, row.index, :, :].rearrange("p t e -> p (t e)"),
                                ps_o[0:P, 0:NT * (1 + E)]).then_inc(s_sgo, 1)

            differences(0)
            average_forward(0)
            average_backward(0)
            both_averages(0, None)

            def iteration(i):
                emb, new, mid, nxt, old, done = (i.plus(k) for k in (4, 3, 2, 1, -1, -2))
                for h in range(NH):
                    if h == 0 and done.exists:
                        dve.wait_ge(s_h2, done.count())
                    if h == 1 and done.exists:
                        dve.wait_ge(s_st2, done.count(NT))
                    if h == 3 and emb.exists:
                        dve.wait_ge(s_st1, emb.count(NT))
                    row, g = (nxt, NH - 1) if h == 0 else (mid, h - 1)
                    if row.exists:
                        score_max(row, g)
                    if h == 0 and nxt.exists:
                        max_parts(nxt)
                    if h == 0 and done.exists:
                        stats(done, lambda t: h_all[0:P, done.index, t * D:(t + 1) * D], st2, s_st2)
                    if h == 1 and done.exists:
                        aggregate(done, st2, mv2, ve2, s_ag2, s_ve2)
                    if h == 1 and new.exists:
                        low(new, parts[:, 0:4:3, :], ps_qk[:, 0:2 * T].rearrange("p (a t) -> p a t", a=2),
                            parts[:, 1:3, :], s_qkh, s_qkl)
                    if h == 2 and emb.exists:
                        dve.wait_ge(s_hin, emb.count())
                        stats(emb, lambda t: h_in[0:P, t, :], st1, s_st1)
                    if h == 2 and precedes_group(emb, U - 1):
                        differences(emb.first // U + 1)
                    if h == 3 and emb.exists:
                        aggregate(emb, st1, mv1, ve1, s_ag1, s_ve1)
                    if h == 3 and precedes_group(emb, U - 1):
                        average_forward(emb.first // U + 1)
                    if h == 4 and old.exists:
                        o_normed(old)
                    if h == 4 and precedes_group(emb, U - 1):
                        average_backward(emb.first // U + 1)
                    if h == 5 and done.exists:
                        low(done, xt_all[:, done.index, 1, :], ps_qk[:, 0:T], xt_all[:, done.index, 0, :],
                            s_x2h, s_x2l)
                    if h == 6 and precedes_group(emb, U - 1):
                        both_averages(emb.first // U + 1, emb)
                    if h == 7 and old.exists:
                        residual(old)
                    if h == 7 and done.exists:
                        router_out(done)

            run_pipeline(dve, iteration)

        @block.tensor
        def _(pe):
            pe.wait_ge(s_w, 16 * 10)
            pe.matmul(ps_in[:, 0:D], w_ve_wide, w_linT, start=True, stop=True)
            pe.wait_ge(s_wv, 4)
            pe.matmul(ps_in[:, D:2 * D], b_ve_wide, w_linT, start=True, stop=True).then_inc(s_pw, 1)
            pe.wait_ge(s_pw, 2 + U)
            pe.wait_ge(s_keep, 2 + 2 * RING)

            def embed(row):
                if row.u == 0:
                    pe.wait_ge(s_smooth, row.first // U * 2 + 1)
                if row.after(1):
                    pe.wait_ge(s_x1e, row.plus(-1).count())
                for t in range(NT):
                    last = pe.matmul(ps_in[0:P, t * D:(t + 1) * D], x_sum[:, t * P:(t + 1) * P],
                                     w_emb[:, row.u, :], start=True, stop=True)
                last.then_inc(s_emb, 1)

            def turn(dst, src):
                for t in range(NT):
                    last = pe.transpose(dst[:, t * P:(t + 1) * P], src(t), identf[0:P, 0:P])
                return last

            def turn_norm1(row):
                if row.after(3):
                    pe.wait_ge(s_mr, row.plus(-3).count())
                pe.wait_ge(s_xn1, row.count(NT))
                turn(ps_in, lambda t: xn1[0:P, t, :]).then_inc(s_x1t, 1)

            def qk(row):
                pe.wait_ge(s_x1e, row.count())
                if row.after(6):
                    pe.wait_ge(s_x2l, row.plus(-6).count())
                elif row.after(1):
                    pe.wait_ge(s_qkl, row.plus(-1).count())
                for a in range(2):
                    last = pe.matmul(ps_qk[:, a * T:(a + 1) * T], w_att[:, a, :], x1t[:], start=True, stop=True)
                last.then_inc(s_qk, 1)

            def values(row):
                if row.after(5):
                    pe.wait_ge(s_h2, row.plus(-5).count())
                elif row.after(1):
                    pe.wait_ge(s_vsb, row.plus(-1).count())
                for t in range(NT):
                    last = pe.matmul(ps_tail[0:P, t * D:(t + 1) * D], x1t[:, t * P:(t + 1) * P], w_att[:, 2, :],
                                     start=True, stop=True)
                last.then_inc(s_v, 1)

            def scores(row, h):
                if h == 0:
                    pe.wait_ge(s_stack[row.u], dma_count(row, 4))
                if h >= 2 or row.after(1):
                    pe.wait_ge(s_max, row.count(NH, h - 1))
                for t in range(NT):
                    last = pe.matmul(ps_s[h % 2][0:P, t * T:(t + 1) * T], head(0, row, h, ROWS_MAX, t * P, P),
                                     head(1, row, h, ROWS_MAX, 0, T), start=True, stop=True)
                last.then_inc(s_s, 1)

            def turn_max(row):
                pe.wait_ge(s_ml, row.count())
                if row.plus(3).exists:
                    pe.wait_ge(s_hraw, row.plus(3).count())
                else:
                    pe.wait_ge(s_mr, row.plus(-1).count())
                pe.transpose(ps_max[0:2 * NH * NT, :], mxp[0:P, :, :].rearrange("p a h -> p (a h)"),
                             identb[0:P, 0:P]).then_inc(s_mt, 1)

            def scores_t(row, h):
                if h == 0:
                    pe.wait_ge(s_mrow[row.u], dma_count(row, 1))
                if h >= 2 or row.after(1):
                    pe.wait_ge(s_exp, row.count(NH, h - 1))
                for t in range(NT):
                    dst = ps_st[h % 2][0:P, t * T:(t + 1) * T]
                    pe.matmul(dst, head(1, row, h, ROWS_ALL, t * P, P), head(0, row, h, ROWS_ALL, 0, T),
                              start=True, stop=True)
                    last = pe.matmul(dst[:, t * P:(t + 1) * P], identb[0:P, 0:P], diag[0:P, t, :],
                                     start=False, stop=True, skip_group_check=True)
                last.then_inc(s_st, 1)

            def weigh(row, g):
                pe.wait_ge(s_exp, row.count(NH, HG * (g + 1)))
                if g == 0:
                    pe.wait_ge(s_vsb, row.count())
                    if row.after(1):
                        pe.wait_ge(s_oev, row.plus(-1).count(2))
                elif row.after(2):
                    pe.wait_ge(s_sgo, row.plus(-2).count())
                else:
                    pe.wait_ge(s_oev, row.count(2, 1))
                for k in range(NT):
                    for j in range(HG):
                        last = pe.matmul(ps_o[CG * j:CG * j + VW, 0:T],
                                         v_sb[0:P, row.u, k, HG * g + j, :], pt[0:P, HG * g + j, k, :],
                                         start=(k == 0), stop=(k == NT - 1))
                last.then_inc(s_pvp, 1)

            def turn_to_tokens(row):
                if row.plus(4).exists:
                    pe.wait_ge(s_vsb, row.plus(4).count())
                else:
                    pe.wait_ge(s_h2, row.plus(-1).count())
                pe.wait_ge(s_oev, row.count(2))
                for t in range(NT):
                    for g in range(2):
                        last = pe.transpose(ps_tail[0:P, (2 * t + g) * D:(2 * t + g + 1) * D],
                                            o_sb[:, g, t * P:(t + 1) * P], identf[:])
                last.then_inc(s_oq, 1)

            def turn_o(row):
                pe.wait_ge(s_on, row.count())
                turn(ps_tail, lambda t: o_n[0:P, t, :, :].rearrange("p h d -> p (h d)")).then_inc(s_ot, 1)

            def project(row):
                pe.wait_ge(s_otb, row.count())
                for t in range(NT):
                    last = pe.matmul(ps_tail[0:P, t * D:(t + 1) * D], ot[:, t * P:(t + 1) * P], w_att[:, 3, :],
                                     start=True, stop=True)
                last.then_inc(s_prj, 1)

            def turn_norm2(row):
                if row.plus(5).exists:
                    pe.wait_ge(s_qkl, row.plus(5).count())
                pe.wait_ge(s_xn2, row.count(NT))
                turn(ps_qk, lambda t: xn2[0:P, t, :]).then_inc(s_x2t, 1)

            def router(row):
                if row.plus(2).exists:
                    pe.wait_ge(s_oev, row.plus(2).count(2, 1))
                else:
                    pe.wait_ge(s_sgo, row.plus(-1).count())
                pe.wait_ge(s_x2l, row.count())
                for t in range(NT):
                    dst = ps_o[0:P, t * (1 + E):(t + 1) * (1 + E)]
                    for n, (part, w) in enumerate(((0, wrh), (0, wrl), (1, wrh))):
                        last = pe.matmul(dst, xt_all[:, row.index, part, t * P:(t + 1) * P], w[:],
                                         start=(n == 0), stop=(n == 2))
                last.then_inc(s_sg, 1)

            def iteration(i):
                emb, new, mid, nxt, old, done = (i.plus(k) for k in (4, 3, 2, 1, -1, -2))
                for h in range(NH):
                    if i.exists:
                        scores_t(i, h)
                    row, g = (nxt, NH - 1) if h == 0 else (mid, h - 1)
                    if row.exists:
                        scores(row, g)
                    if h == 0 and new.exists:
                        qk(new)
                    if h == 1 and old.exists:
                        weigh(old, 1)
                    if h == 1 and emb.exists:
                        embed(emb)
                    if h == 2 and new.exists:
                        values(new)
                    if h == 2 and nxt.exists:
                        turn_max(nxt)
                    if h == 4 and old.exists:
                        turn_to_tokens(old)
                    if h == 4 and i.exists:
                        weigh(i, 0)
                    if h == 4 and done.exists:
                        turn_norm2(done)
                    if h == 5 and old.exists:
                        turn_o(old)
                    if h == 6 and emb.exists:
                        turn_norm1(emb)
                    if h == 7 and old.exists:
                        project(old)
                    if h == 7 and done.exists:
                        router(done)

            run_pipeline(pe, iteration)


def experts_phase(nc, h_all, xt_all, sg_all, identf, attn_b_col, gate_b_row, w1, b1, w2, b2, out):
    with ExitStack() as ctx:
        def sb(name, shape, dt=F32):
            return ctx.enter_context(nc.sbuf_tensor(name, shape, dt))

        def sem(name):
            return ctx.enter_context(nc.semaphore(name))

        def bank(name):
            return ctx.enter_context(nc.psum_tensor(name, [D, 512], F32))

        ps_h = [bank(f"ps_h{i}") for i in range(4)]
        ps_e = [bank(f"ps_e{i}") for i in range(2)]
        ps_y = bank("ps_y")
        ps_r = bank("ps_r")

        w1s = sb("w1s", [D, E, 2, HID], BF16)
        w2s = sb("w2s", [D, E, 2, HC, D], BF16)
        w1f = sb("w1f", [D, STAGE, HID])
        w2f = sb("w2f", [D, STAGE, HC, D])
        b1f = sb("b1f", [E, HID])
        b2f = sb("b2f", [E, D])
        ones = sb("ones", [D, D])
        iota = sb("iota", [B, E])
        small = sb("small", [B, 16])
        tok_wt = sb("tok_wt", [D, NT, B])
        logit = sb("logit", [B, E])
        gate_e = sb("gate_e", [B, E])
        gate = sb("gate", [B, E])
        top = sb("top", [B, 8])
        top_i = sb("top_i", [B, 8], U32)
        top_f = sb("top_f", [B, TOPK])
        weight = sb("weight", [B, TOPK])
        spread = sb("spread", [B, TOPK, B])
        onehot = sb("onehot", [B, TOPK, E])
        onehot_t = sb("onehot_t", [E, TOPK * B])
        chosen = sb("chosen", [1, B * TOPK], U32)
        weight_bc = sb("weight_bc", [D, TOPK, B])
        b1_sel = sb("b1_sel", [D, HC, TOPK, B])
        b2_sel = sb("b2_sel", [D, TOPK, B])
        hid = sb("hid", [D, TOPK, HC, T])
        spare = hid[:].rearrange("p k c t -> p (k c t)")
        tok, tok_e, tok_w = (spare[0:B, i * T:(i + 1) * T] for i in range(3))
        pooled = spare[:, 3 * T:3 * T + NT * B * E].rearrange("p (t b e) -> p t b e", t=NT, b=B)
        hid_h = sb("hid_h", [D, TOPK, HC, T], BF16)
        hid_l = sb("hid_l", [D, TOPK, HC, T], BF16)
        eo = sb("eo", [D, TOPK, T])
        y0 = sb("y0", [D, T])
        y = sb("y", [D, T])
        out_sb = sb("out_sb", [D, NT * D])

        s_c, s_cast = sem("expert_biases"), sem("experts_split")
        s_w = [sem(f"expert_weights{i}") for i in range(STAGE)]
        s_wh, s_cast_ones, s_oh = sem("expert_hi"), sem("router_fills"), sem("choice_spread")
        s_r, s_rv, s_ra, s_idx = sem("router_pe"), sem("router_dve"), sem("router_act"), sem("chosen_ready")
        s_h, s_hid, s_hh, s_hl = sem("hidden"), sem("hidden_gelu"), sem("hidden_hi"), sem("hidden_lo")
        s_e, s_eo, s_y, s_yt, s_o, s_w_out = (sem(n) for n in (
            "expert_out", "expert_gelu", "weighted", "weighted_turned", "out_ready", "out_written"))
        block = ctx.enter_context(nc.Block())

        @block.sync
        def _(sp):
            for e in range(E):
                if e == STAGE:
                    sp.dma_start(b1f[:], b1).then_inc(s_c, 16)
                    sp.dma_start(b2f[:], b2).then_inc(s_c, 16)
                if e >= STAGE:
                    sp.wait_ge(s_cast, 2 * (e - STAGE + 1))
                sp.dma_start(w1f[:, e % STAGE, :], w1[e]).then_inc(s_w[e % STAGE], 16)
                sp.dma_start(w2f[:, e % STAGE, :, :], w2[e].rearrange("(c p) o -> p c o", p=D)).then_inc(s_w[e % STAGE], 16)
            with sp.Fori(0, B, 1) as b:
                sp.wait_ge(s_o, b + 1)
                sp.dma_start(out[b].rearrange("(t p) d -> p t d", p=P),
                             out_sb[0:P, :].rearrange("p (t d) -> p t d", t=NT)).then_inc(s_w_out, 16)
            sp.wait_ge(s_w_out, 16 * B)

        @block.gpsimd
        def _(pool):
            pool.memset(ones[:], 1.0).then_inc(s_cast_ones, 1)
            for e in range(E):
                pool.memset(iota[:, e:e + 1], float(e))
            pool.memset(small[:, 8:9], 0.0).then_inc(s_cast_ones, 1)
            pool.wait_ge(s_rv, 16)
            pool.dma_start(chosen[:], top_i[:, 0:TOPK]).then_inc(s_idx, 16)

        @block.scalar
        def _(act):
            def high(e):
                act.wait_ge(s_w[e % STAGE], 32 * (e // STAGE + 1))
                act.copy(w1s[:, e, 0, :], w1f[:, e % STAGE, :]).then_inc(s_wh, 1)
                act.copy(w2s[:, e, 0, :, :], w2f[:, e % STAGE, :, :]).then_inc(s_wh, 1)

            high(0)
            act.wait_ge(s_rv, 2)
            act.activation(tok_e, tok, ACT.Exp, bias=small[:, 0:1], accum_out=small[:, 1:2]).then_inc(s_ra, 1)
            for e in range(1, 4):
                high(e)
            act.wait_ge(s_rv, 9)
            act.activation(gate_e[:], logit[:], ACT.Exp, bias=small[:, 3:4], accum_out=small[:, 4:5]).then_inc(s_ra, 1)
            for e in range(4, E):
                high(e)

            act.wait_ge(s_cast_ones, 2)
            act.activation(small[:, 10:11], small[:, 8:9], ACT.Gelu)

            def hidden(b, k, s):
                if not isinstance(b, int) or b > 0:
                    act.wait_ge(s_hl, s - 1)
                for half in range(2):
                    act.wait_ge(s_h, s * 2 + half + 1)
                    for j in range(2):
                        c = 2 * half + j
                        last = act.activation(hid[:, k, c, :], ps_h[2 * k + half][:, j * T:(j + 1) * T], ACT.Gelu,
                                              bias=b1_sel[:, c, k, at(b)])
                    last.then_inc(s_hid, 1)

            def output(b, k, s):
                act.wait_ge(s_e, s + 1)
                if not isinstance(b, int) or b > 0:
                    act.wait_ge(s_y, s - 1)
                act.activation(eo[:, k, :], ps_e[k][:, 0:T], ACT.Gelu, bias=b2_sel[:, k, at(b)]).then_inc(s_eo, 1)

            act.wait_ge(s_rv, 19)
            run_steps(act, hidden, output)

        @block.vector
        def _(dve):
            def low(e):
                dve.wait_ge(s_w[e % STAGE], 32 * (e // STAGE + 1))
                dve.wait_ge(s_wh, 2 * (e + 1))
                dve.tensor_tensor(w1s[:, e, 1, :], w1f[:, e % STAGE, :], w1s[:, e, 0, :], ALU.subtract).then_inc(s_cast, 1)
                dve.tensor_tensor(w2s[:, e, 1, :, :], w2f[:, e % STAGE, :, :], w2s[:, e, 0, :, :],
                                  ALU.subtract).then_inc(s_cast, 1)

            dve.wait_ge(s_cast_ones, 2)
            dve.wait_ge(s_r, 1)
            dve.tensor_scalar(tok, ps_r[0:B, 0:T], attn_b_col[:, 0:1], None, ALU.add).then_inc(s_rv, 1)
            dve.wait_ge(s_rv, 1)
            dve.tensor_reduce(small[:, 0:1], tok, AX_X, ALU.max, negate=True).then_inc(s_rv, 1)
            low(0)
            dve.wait_ge(s_ra, 1)
            dve.reciprocal(small[:, 2:3], small[:, 1:2]).then_inc(s_rv, 1)
            dve.wait_ge(s_rv, 3)
            dve.tensor_scalar(tok_w, tok_e, small[:, 2:3], None, ALU.mult).then_inc(s_rv, 1)
            low(1)
            dve.wait_ge(s_r, 2)
            dve.tensor_copy(tok_wt[0:P, :, :], ps_y[0:P, 0:NT * B].rearrange("p (t b) -> p t b", t=NT)).then_inc(s_rv, 1)
            dve.wait_ge(s_rv, 5)
            for t in range(NT):
                wide = tok_wt[0:P, t, :].rearrange("p (b o) -> p b o", o=1).broadcast_to([P, B, E])
                dve.tensor_tensor(pooled[0:P, t, :, :], sg_all[0:P, :, t, 1:1 + E], wide, ALU.mult).then_inc(s_rv, 1)
            low(2)
            low(3)
            dve.wait_ge(s_r, 3)
            dve.tensor_tensor(logit[:], ps_r[0:B, 256:256 + E], gate_b_row[:], ALU.add).then_inc(s_rv, 1)
            dve.wait_ge(s_rv, 8)
            dve.tensor_reduce(small[:, 3:4], logit[:], AX_X, ALU.max, negate=True).then_inc(s_rv, 1)
            dve.wait_ge(s_ra, 2)
            dve.reciprocal(small[:, 5:6], small[:, 4:5]).then_inc(s_rv, 1)
            dve.wait_ge(s_rv, 10)
            dve.tensor_scalar(gate[:], gate_e[:], small[:, 5:6], None, ALU.mult).then_inc(s_rv, 1)
            dve.wait_ge(s_rv, 11)
            dve.max(top[:], gate[:]).then_inc(s_rv, 1)
            dve.wait_ge(s_rv, 12)
            dve.max_index(top_i[:], top[:], gate[:]).then_inc(s_rv, 1)
            dve.tensor_reduce(small[:, 6:7], top[:, 0:TOPK], AX_X, ALU.add).then_inc(s_rv, 1)
            dve.wait_ge(s_rv, 14)
            dve.tensor_scalar(small[:, 7:8], small[:, 6:7], 1e-9, None, ALU.add).then_inc(s_rv, 1)
            dve.tensor_copy(top_f[:], top_i[:, 0:TOPK]).then_inc(s_rv, 1)
            dve.wait_ge(s_rv, 16)
            dve.reciprocal(small[:, 9:10], small[:, 7:8]).then_inc(s_rv, 1)
            for k in range(TOPK):
                last = dve.tensor_scalar(onehot[:, k, :], iota[:], top_f[:, k:k + 1], None, ALU.is_equal)
            last.then_inc(s_oh, 1)
            dve.wait_ge(s_rv, 17)
            dve.tensor_scalar(weight[:], top[:, 0:TOPK], small[:, 9:10], None, ALU.mult).then_inc(s_oh, 1)
            dve.wait_ge(s_oh, 2)
            for k in range(TOPK):
                last = dve.tensor_scalar(spread[:, k, :], identf[0:B, 0:B], weight[:, k:k + 1], None, ALU.mult)
            last.then_inc(s_oh, 1)
            dve.wait_ge(s_r, 4)
            dve.tensor_copy(onehot_t[:], ps_y[0:E, 0:TOPK * B]).then_inc(s_oh, 1)
            low(4)
            low(5)
            dve.wait_ge(s_r, 5)
            dve.tensor_copy(weight_bc[:].rearrange("p k b -> p (k b)"), ps_r[:, 0:TOPK * B]).then_inc(s_oh, 1)
            dve.wait_ge(s_r, 6)
            dve.tensor_copy(b1_sel[:].rearrange("p c k b -> p (c k b)"), ps_y[:, 0:HC * TOPK * B]).then_inc(s_rv, 1)
            dve.tensor_copy(b2_sel[:].rearrange("p k b -> p (k b)"), ps_r[:, 128:128 + TOPK * B]).then_inc(s_rv, 1)
            low(6)
            low(7)

            def hidden(b, k, s):
                dve.wait_ge(s_hid, s * 2 + 2)
                if not isinstance(b, int) or b > 0:
                    dve.wait_ge(s_e, s - 1)
                dve.tensor_copy(hid_h[:, k, :, :], hid[:, k, :, :]).then_inc(s_hh, 1)
                dve.wait_ge(s_hh, s + 1)
                dve.tensor_tensor(hid_l[:, k, :, :], hid[:, k, :, :], hid_h[:, k, :, :], ALU.subtract).then_inc(s_hl, 1)

            def output(b, k, s):
                dve.wait_ge(s_eo, s + 1)
                if k == 0:
                    if not isinstance(b, int) or b > 0:
                        dve.wait_ge(s_y, s)
                    dve.tensor_scalar(y0[:], eo[:, 0, :], weight_bc[:, 0, at(b)], None, ALU.mult).then_inc(s_y, 1)
                    return
                dve.wait_ge(s_y, s)
                if not isinstance(b, int) or b > 0:
                    dve.wait_ge(s_yt, b)
                dve.scalar_tensor_tensor(y[:], eo[:, 1, :], weight_bc[:, 1, at(b)], y0[:], ALU.mult,
                                         ALU.add).then_inc(s_y, 1)

            def finish(b):
                dve.wait_ge(s_yt, b + 1)
                if not isinstance(b, int) or b > 0:
                    dve.wait_ge(s_w_out, 16 * b)
                dve.tensor_tensor(out_sb[0:P, :], ps_y[0:P, 0:NT * D], h_all[0:P, b, :], ALU.add).then_inc(s_o, 1)

            run_steps(dve, hidden, output, finish)

        @block.tensor
        def _(pe):
            pe.wait_ge(s_cast_ones, 2)
            for t in range(NT):
                last = pe.transpose(ps_r[0:B, t * P:(t + 1) * P], sg_all[0:P, :, t, 0], identf[0:P, 0:P])
            last.then_inc(s_r, 1)
            pe.wait_ge(s_rv, 4)
            for t in range(NT):
                last = pe.transpose(ps_y[0:P, t * B:(t + 1) * B], tok_w[:, t * P:(t + 1) * P], identf[0:B, 0:B])
            last.then_inc(s_r, 1)
            pe.wait_ge(s_rv, 7)
            for e in range(E):
                for t in range(NT):
                    last = pe.matmul(ps_r[0:B, 256 + e:257 + e], pooled[0:P, t, :, e], ones[0:P, 0:1],
                                     start=(t == 0), stop=(t == NT - 1))
            last.then_inc(s_r, 1)
            pe.wait_ge(s_oh, 1)
            for k in range(TOPK):
                last = pe.transpose(ps_y[0:E, k * B:(k + 1) * B], onehot[:, k, :], identf[0:B, 0:B])
            last.then_inc(s_r, 1)
            pe.wait_ge(s_oh, 3)
            for k in range(TOPK):
                last = pe.matmul(ps_r[:, k * B:(k + 1) * B], ones[0:B, :], spread[:, k, :], start=True, stop=True)
            last.then_inc(s_r, 1)
            pe.wait_ge(s_oh, 5)
            pe.wait_ge(s_c, 16 * 2)
            for c in range(HC):
                pe.matmul(ps_y[:, c * TOPK * B:(c + 1) * TOPK * B], b1f[:, c * D:(c + 1) * D], onehot_t[:],
                          start=True, stop=True)
            pe.matmul(ps_r[:, 128:128 + TOPK * B], b2f[:], onehot_t[:], start=True, stop=True).then_inc(s_r, 1)
            pe.wait_ge(s_rv, 19)
            pe.wait_ge(s_cast, 2 * E)
            pe.wait_ge(s_idx, 16)

            def load_choices(s, n):
                place = chosen[0:1, s:s + n] if isinstance(s, int) else chosen[0:1, bass.ds(s, n)]
                return nc.values_load_multi_w_load_instructions(
                    place, engines=[mybir.EngineType.PE], min_val=0, max_val=E - 1,
                    skip_runtime_bounds_check_because="they are max_index's places among E columns")[1]

            def hidden(b, k, s, e):
                if not isinstance(b, int) or b > 0:
                    pe.wait_ge(s_hid, s * 2 - 2)
                for half in range(2):
                    for j in range(2):
                        c = 2 * half + j
                        dst = ps_h[2 * k + half][:, j * T:(j + 1) * T]
                        for n, (wp, xp) in enumerate(((0, 0), (0, 1), (1, 0))):
                            last = pe.matmul(dst, w1s[:, e, wp, c * D:(c + 1) * D], xt_all[:, b, xp, :],
                                             start=(n == 0), stop=(n == 2))
                    last.then_inc(s_h, 1)

            def output(b, k, s, e):
                pe.wait_ge(s_hl, s + 1)
                if not isinstance(b, int) or b > 0:
                    pe.wait_ge(s_eo, s - 1)
                for c in range(HC):
                    for n, (wp, part) in enumerate(((0, hid_h), (0, hid_l), (1, hid_h))):
                        last = pe.matmul(ps_e[k][:, 0:T], w2s[:, e, wp, c, :], part[:, k, c, :],
                                         start=(c == 0 and n == 0), stop=(c == HC - 1 and n == 2))
                last.then_inc(s_e, 1)

            def finish(b):
                pe.wait_ge(s_y, b * 2 + 2)
                if not isinstance(b, int) or b > 0:
                    pe.wait_ge(s_o, b)
                for t in range(NT):
                    last = pe.transpose(ps_y[0:P, t * D:(t + 1) * D], y[:, t * P:(t + 1) * P], identf[:])
                last.then_inc(s_yt, 1)

            run_steps(pe, hidden, output, finish, load_choices)


def at(i):
    return slice(i, i + 1) if isinstance(i, int) else bass.ds(i, 1)


def run_steps(eng, hidden, output, finish=None, load_choices=None):
    def chosen(s, n):
        return [(e,) for e in load_choices(s, n)] if load_choices is not None else [()] * n

    def row(b, e, first=False, last=False):
        for k in range(TOPK):
            if not last:
                hidden(b + 1, k, b * 2 + 2 + k, *e[TOPK + k])
            output(b, k, b * 2 + k, *e[k])
            if k == 0 and finish is not None and not first:
                finish(b - 1)

    e = chosen(0, TOPK)
    for k in range(TOPK):
        hidden(0, k, k, *e[k])
    peeled = 1 + (B - 2) % ROWS_C
    for b in range(peeled):
        row(b, chosen(b * 2, 2 * TOPK), first=(b == 0))
    with eng.Fori(0, (B - 1 - peeled) // ROWS_C, 1) as trip:
        b = trip * ROWS_C + peeled
        e = chosen(b * 2, (ROWS_C + 1) * TOPK)
        for r in range(ROWS_C):
            row(b + r, e[r * TOPK:])
    row(B - 1, chosen(2 * B - 2, TOPK), last=True)
    if finish is not None:
        finish(B - 1)


def bass_audio_tower(nc, consts, x, W_ve, W_lin_T, b_ve, b_lin, w_qkv_T, w_out_T, b_out,
                     attn_w, attn_b, gate_w, gate_b, w1, b1, w2, b2, out):
    with ExitStack() as ctx:
        h_all = ctx.enter_context(nc.sbuf_tensor("h_all", [D, B, NT * D], F32))
        xt_all = ctx.enter_context(nc.sbuf_tensor("xt_all", [D, B, 2, T], BF16))
        sg_all = ctx.enter_context(nc.sbuf_tensor("sg_all", [D, B, NT, 1 + E], F32))
        identf = ctx.enter_context(nc.sbuf_tensor("identf", [D, D], F32))
        attn_b_col = ctx.enter_context(nc.sbuf_tensor("attn_b_col", [B, 1], F32))
        gate_b_row = ctx.enter_context(nc.sbuf_tensor("gate_b_row", [B, E], F32))
        attention_phase(nc, h_all, xt_all, sg_all, identf, attn_b_col, gate_b_row, consts, x, W_ve, W_lin_T,
                        b_ve, b_lin, w_qkv_T, w_out_T, b_out, attn_w, attn_b, gate_w, gate_b)
        experts_phase(nc, h_all, xt_all, sg_all, identf, attn_b_col, gate_b_row, w1, b1, w2, b2, out)


def kernel(x, L0_tok_W_ve, L0_tok_b_ve, L0_tok_W_lin, L0_tok_b_lin, L0_attn_w_qkv, L0_attn_w_out,
           L0_attn_b_out, L0_ffn_attn_w, L0_ffn_attn_b, L0_ffn_gate_w, L0_ffn_gate_b, L0_ffn_w1,
           L0_ffn_b1, L0_ffn_w2, L0_ffn_b2):
    import concourse.bacc as bacc
    from concourse.bass_utils import run_bass_kernel_spmd

    qkv = np.asarray(L0_attn_w_qkv)
    qk = qkv[:2 * D].reshape(2, NH, HD, D).transpose(0, 2, 1, 3).reshape(2 * D, D)
    qkv_T = np.concatenate([qk, qkv[2 * D:]]).T

    laid_out = {
        "consts": constants(), "x": x, "W_ve": L0_tok_W_ve, "W_lin_T": np.asarray(L0_tok_W_lin).T,
        "b_ve": L0_tok_b_ve, "b_lin": L0_tok_b_lin, "w_qkv_T": qkv_T,
        "w_out_T": np.asarray(L0_attn_w_out).T, "b_out": L0_attn_b_out, "attn_w": L0_ffn_attn_w,
        "attn_b": L0_ffn_attn_b, "gate_w": L0_ffn_gate_w, "gate_b": L0_ffn_gate_b, "w1": L0_ffn_w1,
        "b1": L0_ffn_b1, "w2": L0_ffn_w2, "b2": L0_ffn_b2,
    }
    nc = bacc.Bacc("TRN2", target_bir_lowering=False, num_devices=1)
    arrays, args = {}, []
    for name, a in laid_out.items():
        a = np.ascontiguousarray(a)
        arrays[f"in_{name}"] = a
        args.append(nc.dram_tensor(f"in_{name}", a.shape, mybir.dt.from_np(a.dtype), kind="ExternalInput").ap())
    args.append(nc.dram_tensor("out_h", (B, T, D), F32, kind="ExternalOutput").ap())
    bass_audio_tower(nc, *args)
    got = run_bass_kernel_spmd(nc, [arrays], core_ids=[0])
    return got.results[0]["out_h"]
```
